# Optimizing a Trainium2 kernel written in Bass

```python
import numpy as np
import jax
import jax.numpy as jnp

def _softmax(x, axis=-1):
    return jax.nn.softmax(x, axis=axis)

def _gelu(x):
    return jax.nn.gelu(x, approximate=True)

def _silu(x):
    return jax.nn.silu(x)

def _sigmoid(x):
    return jax.nn.sigmoid(x)

def _layernorm(x, axis=-1, eps=1e-05):
    m = jnp.mean(x, axis=axis, keepdims=True)
    v = jnp.var(x, axis=axis, keepdims=True)
    return (x - m) / jnp.sqrt(v + eps)

def _scatter_add(tgt, idx, src, axis=0):
    return tgt.at[idx].add(src)

def _segment_sum(src, seg, n):
    return jax.ops.segment_sum(src, seg, n)
kernel_name = 'mk_conv_attn_hybrid_d2_conv_nchw512_r4_aa1917'

def setup_inputs(seed: int=0):
    np.random.seed(seed)
    _w = jnp.asarray

    def _rec_inputs():
        import jax
        import jax.numpy as jnp
        _gk = jax.random.key(seed)
        x = 7.22e-05 + 1 * jax.random.normal(jax.random.fold_in(_gk, 1), (4, 128, 16, 16), jnp.float32)
        return x
    x = _rec_inputs()

    def _L0_conv_setup():
        import jax, jax.numpy as jnp
        import numpy as np
        EPS = 1e-05

        def conv1x1(x, w, b):
            return jnp.einsum('bchw,oc->bohw', x, w) + b[None, :, None, None]

        def bn_eval(x, gamma, beta, mean, var):
            inv = gamma / jnp.sqrt(var + EPS)
            return x * inv[None, :, None, None] + (beta - mean * inv)[None, :, None, None]
        key = jax.random.key(seed)
        ks = jax.random.split(key, 20)
        B, C, H, W = (4, 128, 16, 16)
        mid = C // 4
        s_in = 1.0 / np.sqrt(C)
        s_mid = 1.0 / np.sqrt(mid)
        inp = {'x': jax.random.normal(ks[0], (B, C, H, W), jnp.float32), 'wf': jax.random.normal(ks[1], (mid, C), jnp.float32) * s_in, 'bf': jnp.zeros((mid,), jnp.float32), 'gf': jnp.ones((mid,), jnp.float32), 'betaf': jnp.zeros((mid,), jnp.float32), 'mf': jax.random.normal(ks[2], (mid,), jnp.float32) * 0.1, 'vf': jax.random.uniform(ks[3], (mid,), jnp.float32) + 0.5, 'wg': jax.random.normal(ks[4], (mid, C), jnp.float32) * s_in, 'bg': jnp.zeros((mid,), jnp.float32), 'gg': jnp.ones((mid,), jnp.float32), 'betag': jnp.zeros((mid,), jnp.float32), 'mg': jax.random.normal(ks[5], (mid,), jnp.float32) * 0.1, 'vg': jax.random.uniform(ks[6], (mid,), jnp.float32) + 0.5, 'wh': jax.random.normal(ks[7], (mid, C), jnp.float32) * s_in, 'bh': jnp.zeros((mid,), jnp.float32), 'wv': jax.random.normal(ks[8], (C, mid), jnp.float32) * s_mid, 'bv': jnp.zeros((C,), jnp.float32)}
        return inp
    _L0_conv_all = _L0_conv_setup()
    _L0_conv_in = {k: v for k, v in _L0_conv_all.items() if k in ('wf', 'bf', 'gf', 'betaf', 'mf', 'vf', 'wg', 'bg', 'gg', 'betag', 'mg', 'vg', 'wh', 'bh', 'wv', 'bv')}
    del _L0_conv_all

    def _L1_attn_setup():
        import jax, jax.numpy as jnp
        import numpy as np
        B, T, D, K, V = (4, 1024, 128, 128, 128)
        key = jax.random.key(seed)
        ks = jax.random.split(key, 7)
        w = lambda k, shp: jax.random.normal(k, shp, dtype=jnp.float32) * 0.02
        return {'minibatch': jax.random.normal(ks[0], (B, T, D), dtype=jnp.float32), 'Wk': w(ks[1], (D, K)), 'bk': jnp.zeros((K,), jnp.float32), 'Wq': w(ks[2], (D, K)), 'bq': jnp.zeros((K,), jnp.float32), 'Wv': w(ks[3], (D, V)), 'bv': jnp.zeros((V,), jnp.float32)}
    _L1_attn_all = _L1_attn_setup()
    _L1_attn_in = {k: v for k, v in _L1_attn_all.items() if k in ('Wk', 'bk', 'Wq', 'bq', 'Wv', 'bv')}
    del _L1_attn_all

    def _L1_ffn_setup():
        import jax, jax.numpy as jnp
        import numpy as np
        D_MODEL = 128
        D_FF = 512
        NUM_EXPERTS = 8
        TOP_K = 2
        key = jax.random.key(seed)
        k_x, k_g, k_w1, k_w2 = jax.random.split(key, 4)
        x = jax.random.normal(k_x, (8, 1024, D_MODEL), dtype=jnp.float32)
        Wg = jax.random.normal(k_g, (D_MODEL, NUM_EXPERTS), dtype=jnp.float32) * (1.0 / np.sqrt(D_MODEL))
        W1 = jax.random.normal(k_w1, (NUM_EXPERTS, D_MODEL, D_FF), dtype=jnp.float32) * (1.0 / np.sqrt(D_MODEL))
        W2 = jax.random.normal(k_w2, (NUM_EXPERTS, D_FF, D_MODEL), dtype=jnp.float32) * (1.0 / np.sqrt(D_FF))
        return {'x': x, 'Wg': Wg, 'W1': W1, 'W2': W2}
    _L1_ffn_all = _L1_ffn_setup()
    _L1_ffn_in = {k: v for k, v in _L1_ffn_all.items() if k in ('Wg', 'W1', 'W2')}
    del _L1_ffn_all
    return {'x': x, 'L0_conv_wf': _L0_conv_in['wf'], 'L0_conv_bf': _L0_conv_in['bf'], 'L0_conv_gf': _L0_conv_in['gf'], 'L0_conv_betaf': _L0_conv_in['betaf'], 'L0_conv_mf': _L0_conv_in['mf'], 'L0_conv_vf': _L0_conv_in['vf'], 'L0_conv_wg': _L0_conv_in['wg'], 'L0_conv_bg': _L0_conv_in['bg'], 'L0_conv_gg': _L0_conv_in['gg'], 'L0_conv_betag': _L0_conv_in['betag'], 'L0_conv_mg': _L0_conv_in['mg'], 'L0_conv_vg': _L0_conv_in['vg'], 'L0_conv_wh': _L0_conv_in['wh'], 'L0_conv_bh': _L0_conv_in['bh'], 'L0_conv_wv': _L0_conv_in['wv'], 'L0_conv_bv': _L0_conv_in['bv'], 'L1_attn_Wk': _L1_attn_in['Wk'], 'L1_attn_bk': _L1_attn_in['bk'], 'L1_attn_Wq': _L1_attn_in['Wq'], 'L1_attn_bq': _L1_attn_in['bq'], 'L1_attn_Wv': _L1_attn_in['Wv'], 'L1_attn_bv': _L1_attn_in['bv'], 'L1_ffn_Wg': _L1_ffn_in['Wg'], 'L1_ffn_W1': _L1_ffn_in['W1'], 'L1_ffn_W2': _L1_ffn_in['W2']}

def reference(x, L0_conv_wf, L0_conv_bf, L0_conv_gf, L0_conv_betaf, L0_conv_mf, L0_conv_vf, L0_conv_wg, L0_conv_bg, L0_conv_gg, L0_conv_betag, L0_conv_mg, L0_conv_vg, L0_conv_wh, L0_conv_bh, L0_conv_wv, L0_conv_bv, L1_attn_Wk, L1_attn_bk, L1_attn_Wq, L1_attn_bq, L1_attn_Wv, L1_attn_bv, L1_ffn_Wg, L1_ffn_W1, L1_ffn_W2):
    import jax
    import jax.numpy as jnp

    def _L0_conv_ref(x, wf, bf, gf, betaf, mf, vf, wg, bg, gg, betag, mg, vg, wh, bh, wv, bv):
        import jax, jax.numpy as jnp
        import numpy as np
        EPS = 1e-05

        def conv1x1(x, w, b):
            return jnp.einsum('bchw,oc->bohw', x, w) + b[None, :, None, None]

        def bn_eval(x, gamma, beta, mean, var):
            inv = gamma / jnp.sqrt(var + EPS)
            return x * inv[None, :, None, None] + (beta - mean * inv)[None, :, None, None]
        B, C, H, W = x.shape
        mid = wf.shape[0]
        HW = H * W
        f_x = jax.nn.relu(bn_eval(conv1x1(x, wf, bf), gf, betaf, mf, vf)).reshape(B, mid, HW)
        g_x = jax.nn.relu(bn_eval(conv1x1(x, wg, bg), gg, betag, mg, vg)).reshape(B, mid, HW)
        h_x = conv1x1(x, wh, bh).reshape(B, mid, HW)
        scale = mid ** (-0.5)
        scores = jnp.einsum('bcn,bcm->bnm', f_x, g_x) * scale
        attn = jax.nn.softmax(scores, axis=-1)
        z = jnp.einsum('bnm,bcm->bcn', attn, h_x).reshape(B, mid, H, W)
        z = conv1x1(z, wv, bv)
        return z + x

    def _L1_attn_ref(minibatch, Wk, bk, Wq, bq, Wv, bv):
        import jax, jax.numpy as jnp
        import numpy as np
        B, T, D, K, V = (4, 1024, 128, 128, 128)
        keys = minibatch @ Wk + bk
        queries = minibatch @ Wq + bq
        values = minibatch @ Wv + bv
        logits = jnp.einsum('btk,bsk->bts', queries, keys)
        t = logits.shape[1]
        mask = jnp.triu(jnp.ones((t, t), dtype=bool), k=1)
        logits = jnp.where(mask[None, :, :], -jnp.inf, logits)
        sqrt_k = jnp.asarray(np.sqrt(K), dtype=logits.dtype)
        probs = jax.nn.softmax(logits, axis=1) / sqrt_k
        read = jnp.einsum('bts,bsv->btv', probs, values)
        return minibatch + read

    def _L1_ffn_ref(x, Wg, W1, W2):
        import jax, jax.numpy as jnp
        import numpy as np
        D_MODEL = 128
        D_FF = 512
        NUM_EXPERTS = 8
        TOP_K = 2
        B, S, D = x.shape
        E = Wg.shape[-1]
        router_logits = jnp.einsum('bsd,de->bse', x, Wg)
        top_logits, top_idx = jax.lax.top_k(router_logits, TOP_K)
        top_w = jax.nn.softmax(top_logits, axis=-1)
        combine = jnp.sum(jax.nn.one_hot(top_idx, E, dtype=x.dtype) * top_w[..., None], axis=-2)
        xt = x.reshape(B * S, D)
        cw = combine.reshape(B * S, E)
        out = jnp.zeros_like(xt)
        for e in range(E):
            h = jax.nn.silu(xt @ W1[e]) @ W2[e]
            out = out + cw[:, e:e + 1] * h
        return out.reshape(B, S, D)

    def _gn(v, G=32, eps=1e-05):
        B_, C_, H_, W_ = v.shape
        g = v.reshape(B_, G, C_ // G, H_, W_)
        m = jnp.mean(g, axis=(2, 3, 4), keepdims=True)
        s = jnp.var(g, axis=(2, 3, 4), keepdims=True)
        return ((g - m) / jnp.sqrt(s + eps)).reshape(v.shape)

    def _ln_c(v, eps=1e-06):
        m = jnp.mean(v, axis=1, keepdims=True)
        s = jnp.var(v, axis=1, keepdims=True)
        return (v - m) / jnp.sqrt(s + eps)

    def _ln_t(v, eps=1e-05):
        m = jnp.mean(v, axis=-1, keepdims=True)
        s = jnp.var(v, axis=-1, keepdims=True)
        return (v - m) / jnp.sqrt(s + eps)

    def _to_tokens(v):
        B_, C_, H_, W_ = v.shape
        return v.reshape(B_, C_, H_ * W_).transpose(0, 2, 1)

    def _from_tokens(t, like):
        B_, C_, H_, W_ = like.shape
        return t.transpose(0, 2, 1).reshape(B_, C_, H_, W_)
    x = _L0_conv_ref(x, L0_conv_wf, L0_conv_bf, L0_conv_gf, L0_conv_betaf, L0_conv_mf, L0_conv_vf, L0_conv_wg, L0_conv_bg, L0_conv_gg, L0_conv_betag, L0_conv_mg, L0_conv_vg, L0_conv_wh, L0_conv_bh, L0_conv_wv, L0_conv_bv)
    t = _to_tokens(x)
    t = t + _L1_attn_ref(_ln_t(t), L1_attn_Wk, L1_attn_bk, L1_attn_Wq, L1_attn_bq, L1_attn_Wv, L1_attn_bv)
    t = t + _L1_ffn_ref(_ln_t(t), L1_ffn_Wg, L1_ffn_W1, L1_ffn_W2)
    x = _from_tokens(t, x)
    return x

_drawn_inputs = setup_inputs


def setup_inputs(seed=0):
    import zlib

    import numpy as np

    out = dict(_drawn_inputs(seed))
    spreads = {'L0_conv_bf': (0.0, 0.443),
     'L0_conv_gf': (1.0, 0.6),
     'L0_conv_betaf': (0.0, 0.561),
     'L0_conv_bg': (0.0, 0.666),
     'L0_conv_gg': (1.0, 0.57),
     'L0_conv_betag': (0.0, 0.573),
     'L0_conv_bh': (0.0, 0.1),
     'L0_conv_bv': (0.0, 0.1),
     'L1_attn_bk': (0.0, 0.718),
     'L1_attn_bq': (0.0, 0.8),
     'L1_attn_bv': (0.0, 0.446)}
    factors = {'L0_conv_mf': 3.977,
     'L0_conv_mg': 3.78,
     'L1_attn_Wk': 8.0,
     'L1_attn_Wq': 7.03,
     'L1_attn_Wv': 5.639}
    for name, (base, spread) in spreads.items():
        noise = np.random.default_rng([zlib.crc32(name.encode()), seed]).standard_normal(out[name].shape)
        drawn = base * np.exp(spread * noise) if base else spread * noise
        out[name] = jnp.asarray(drawn.astype(out[name].dtype))
    for name, factor in factors.items():
        out[name] = (out[name] * factor).astype(out[name].dtype)
    return out
```

```python
import concourse.bass as bass
from concourse import mybir
from contextlib import ExitStack


def conv_attention_moe_kernel(
    nc: bass.Bass,
    x: bass.AP,
    wf: bass.AP, bf: bass.AP, gf: bass.AP, betaf: bass.AP, mf: bass.AP, vf: bass.AP,
    wg: bass.AP, bg: bass.AP, gg: bass.AP, betag: bass.AP, mg: bass.AP, vg: bass.AP,
    wh: bass.AP, bh: bass.AP, wv: bass.AP, bv: bass.AP,
    Wk: bass.AP, bk: bass.AP, Wq: bass.AP, bq: bass.AP, Wv: bass.AP, bvalue: bass.AP,
    Wgate: bass.AP, W1: bass.AP, W2: bass.AP,
    out: bass.AP,
):
    fp32 = mybir.dt.float32
    fp16 = mybir.dt.float16
    bf16 = mybir.dt.bfloat16
    u32 = mybir.dt.uint32
    ALU = mybir.AluOpType
    ACT = mybir.ActivationFunctionType
    AX = mybir.AxisListType

    B, C, H, W = x.shape
    N = H * W
    P = 128
    A = N // P
    T = B * A
    MID = wf.shape[0]
    E, _, F = W1.shape
    FC = F // P
    NG = 2
    GB = B // NG
    GT = T // NG
    GN = GT * P
    TOPS = 8
    BN_EPS = 1e-5
    LN_EPS = 1e-5
    NEG = -1e30
    XS = 16.0
    WS = 256.0
    CS = 64.0
    NP = 13
    R_BK, R_BQ, R_BH = 10, 11, 12

    x_v = x.rearrange("b c h w -> c b (h w)")
    out_v = out.rearrange("b c h w -> c b (h w)")

    def row(v, n=1):
        return v.rearrange("(a n) -> a n", a=n)

    def four(v):
        return row(v).unsqueeze(1).broadcast_to([1, B, MID])

    ctx = ExitStack()
    with ctx:
        def sb(name, shape, dt=fp32):
            return ctx.enter_context(nc.sbuf_tensor(name, shape, dt))

        def sem(name):
            return ctx.enter_context(nc.semaphore(name))

        xT = sb("xT", [P, B, N])
        rows = sb("rows", [NP, P])
        rows4 = rows[:, :].rearrange("p (b m) -> p b m", b=B)
        cols = sb("cols", [P, NP])
        wf_s = sb("wf_s", [MID, P])
        wg_s = sb("wg_s", [MID, P])
        wh_s = sb("wh_s", [MID, P])
        wv_s = sb("wv_s", [P, MID])
        wfT = sb("wfT", [P, 2 * MID])
        wvT = sb("wvT", [MID, P])
        bh_wide = sb("bh_wide", [MID, P])
        bv_row = sb("bv_row", [1, P])
        bvalue_row = sb("bvalue_row", [1, P])
        fold = sb("fold", [P, 3, P])
        ident = sb("ident", [P, P])
        identb = sb("identb", [P, P], bf16)
        maskb = sb("maskb", [P, P], bf16)
        ones = sb("ones", [P, P])
        sel = sb("sel", [P, E, P], fp16)
        iota_e = sb("iota_e", [P, E])
        power = sb("power", [P, T])
        qscale = sb("qscale", [P, 2])
        bn_var = sb("bn_var", [P, 2])
        bn_inv = sb("bn_inv", [P, 2])
        bn_scale = sb("bn_scale", [P, 2])
        bn_tmp = sb("bn_tmp", [P, 2])
        bn_beta = sb("bn_beta", [P, 2])
        bn_bias = sb("bn_bias", [P, 2])
        fg = sb("fg", [P, 2, N])
        hv = sb("hv", [P, T, P])
        xb = sb("xb", [P, T, P])
        nmax0 = sb("nmax0", [P, T])
        sum0 = sb("sum0", [P, T])
        rec0 = sb("rec0", [P, T])
        prob0 = sb("prob0", [P, T, N])
        prob0T = sb("prob0T", [P, T, N])
        t0 = sb("t0", [P, T, P])
        st0 = sb("st0", [P, T, 6])
        mv0 = sb("mv0", [P, T, 2])
        ve0 = sb("ve0", [P, T])
        rstd0 = sb("rstd0", [P, T])
        y = sb("y", [P, T, P])
        ty = sb("ty", [P, T, P])
        yT = sb("yT", [P, B, N])
        Wk_s = sb("Wk_s", [P, P])
        Wq_s = sb("Wq_s", [P, P])
        Wv_s = sb("Wv_s", [P, P])
        Wgate_s = sb("Wgate_s", [P, E])
        kT = sb("kT", [P, B, N])
        qT = sb("qT", [P, B, N])
        val = sb("val", [P, T, P])
        vals = sb("vals", [P, T, P])
        LW = N + (A - 1) * P
        nmax1 = sb("nmax1", [P, T])
        sum1 = sb("sum1", [P, T])
        rec1 = sb("rec1", [P, T])
        prob1 = sb("prob1", [P, B, LW])
        t1 = sb("t1", [P, T, P])
        st1 = sb("st1", [P, T, 6])
        mv1 = sb("mv1", [P, T, 2])
        ve1 = sb("ve1", [P, T])
        rstd1 = sb("rstd1", [P, T])
        z = sb("z", [P, T, P])
        zT = sb("zT", [P, B, N])
        acc = sb("acc", [P, B, N])
        zh = sb("zh", [P, B, N], fp16)
        zl = sb("zl", [P, B, N], fp16)
        rl = sb("rl", [P, T, E])
        top = sb("top", [P, T, TOPS])
        topi = sb("topi", [P, T, TOPS], u32)
        topf = sb("topf", [P, T, 2])
        gap = sb("gap", [P, T, 1])
        e2 = sb("e2", [P, T, 1])
        den = sb("den", [P, T, 1])
        g1 = sb("g1", [P, T, 1])
        g2 = sb("g2", [P, T, 1])
        oh1 = sb("oh1", [P, T, E])
        oh2 = sb("oh2", [P, T, E])
        gw1 = sb("gw1", [P, T, E])
        gw2 = sb("gw2", [P, T, E])
        gate = sb("gate", [P, T, E])
        gateh = sb("gateh", [P, NG, GN], fp16)
        gatel = sb("gatel", [P, NG, GN], fp16)
        gatew = sb("gatew", [P, 2, GN])
        W1f = sb("W1f", [P, E, F])
        W2f = sb("W2f", [P, E, F])
        W1h = sb("W1h", [P, E, F], fp16)
        W1l = sb("W1l", [P, E, F], fp16)
        W2h = sb("W2h", [P, E, F], fp16)
        W2l = sb("W2l", [P, E, F], fp16)
        HB = 4
        hid = sb("hid", [P, HB, GN])
        hidh = sb("hidh", [P, HB, GN], fp16)
        hidl = sb("hidl", [P, HB, GN], fp16)
        gated = sb("gated", [P, 2, GN])

        bank = [ctx.enter_context(nc.psum_tensor(f"bank{i}", [P, 512], fp32)) for i in range(8)]
        pFG = bank[0]
        pHV = [bank[1], bank[2]]
        pX = [bank[3], bank[4]]
        pFOLD = bank[5]
        pSET = bank[6]
        ringA = [bank[5], bank[6], bank[7], bank[0]]
        ringB = [bank[1], bank[2], bank[3], bank[4]]
        pS = pU = pKQ = pL = pZ = ringA
        pPT = pYT = pV = pR = ringB
        pRT = [bank[1], bank[2]]
        pCT = [bank[3], bank[4]]
        pUP = ringA
        pDN = [bank[1], bank[2]]
        pGW = [bank[3], bank[4]]

        x_in = [sem(f"x_in{b}") for b in range(B)]
        rows_in = sem("rows_in")
        convw_in = sem("convw_in")
        attnw_in = sem("attnw_in")
        w1_in = [sem(f"w1_in{e}") for e in range(E)]
        w2_in = [sem(f"w2_in{e}") for e in range(E)]
        zero_set = sem("zero_set")
        ident_set = sem("ident_set")
        mask_set = sem("mask_set")
        ones_set = sem("ones_set")
        consts_set = sem("consts_set")
        sel_set = sem("sel_set")
        gate_zeroed = sem("gate_zeroed")
        setup_T = sem("setup_T")
        setup_copied = sem("setup_copied")
        bh_widened = sem("bh_widened")
        fold_done = sem("fold_done")
        fold_copied = sem("fold_copied")
        bn_v = sem("bn_v")
        bn_ready = sem("bn_ready")
        xT_done = sem("xT_done")
        xb_ready = sem("xb_ready")
        fg_done = sem("fg_done")
        fg_ready = sem("fg_ready")
        hv_done = sem("hv_done")
        hv_ready = sem("hv_ready")
        s_done = sem("s_done")
        nmax0_ready = sem("nmax0_ready")
        prob0_ready = sem("prob0_ready")
        rec0_ready = sem("rec0_ready")
        pT_done = sem("pT_done")
        prob0T_ready = sem("prob0T_ready")
        u_done = sem("u_done")
        t0_ready = sem("t0_ready")
        st0_ready = sem("st0_ready")
        mv0_ready = sem("mv0_ready")
        ve0_ready = sem("ve0_ready")
        rstd0_ready = sem("rstd0_ready")
        y_ready = sem("y_ready")
        ty_ready = sem("ty_ready")
        yT_done = sem("yT_done")
        yT_ready = sem("yT_ready")
        kq_done = sem("kq_done")
        kq_ready = sem("kq_ready")
        v_done = sem("v_done")
        val_ready = sem("val_ready")
        l_done = sem("l_done")
        nmax1_ready = sem("nmax1_ready")
        prob1_ready = sem("prob1_ready")
        rec1_ready = sem("rec1_ready")
        vals_ready = sem("vals_ready")
        r_done = sem("r_done")
        t1_ready = sem("t1_ready")
        st1_ready = sem("st1_ready")
        mv1_ready = sem("mv1_ready")
        ve1_ready = sem("ve1_ready")
        rstd1_ready = sem("rstd1_ready")
        z_ready = sem("z_ready")
        zT_done = sem("zT_done")
        zT_ready = sem("zT_ready")
        acc_ready = sem("acc_ready")
        zh_ready = sem("zh_ready")
        zl_ready = sem("zl_ready")
        rt_done = sem("rt_done")
        rl_ready = sem("rl_ready")
        top_ready = sem("top_ready")
        topi_ready = sem("topi_ready")
        topf_ready = sem("topf_ready")
        gap_ready = sem("gap_ready")
        e2_ready = sem("e2_ready")
        den_ready = sem("den_ready")
        g1_ready = sem("g1_ready")
        g2_ready = sem("g2_ready")
        oh_ready = sem("oh_ready")
        gw_ready = sem("gw_ready")
        gate_ready = sem("gate_ready")
        gateT_done = sem("gateT_done")
        gateh_ready = sem("gateh_ready")
        gatel_ready = sem("gatel_ready")
        wh_ready = sem("wh_ready")
        wl_ready = sem("wl_ready")
        up_done = sem("up_done")
        hid_ready = sem("hid_ready")
        hidh_ready = sem("hidh_ready")
        hidl_even = sem("hidl_even")
        hidl_odd = sem("hidl_odd")
        down_done = sem("down_done")
        gw_done = sem("gw_done")
        gatew_ready = sem("gatew_ready")
        gated_ready = sem("gated_ready")
        acc_added = sem("acc_added")
        out_stored = sem("out_stored")

        block = ctx.enter_context(nc.Block())

        U = NG * FC
        UNITS = E * U
        SUMS = E * NG
        LAG = 3

        def per_expert(eng, steps, tail):
            steps(0, True, False)
            with eng.Fori(1, E - 1) as e:
                steps(e, False, False)
            steps(E - 1, False, True)
            tail()

        @block.sync
        def _(sync):
            sync.dma_start(xT[:, 0, :], x_v[:, 0, :]).then_inc(x_in[0], 16)
            sync.dma_start(wf_s[:, :], wf).then_inc(convw_in, 16)
            sync.dma_start(wg_s[:, :], wg).then_inc(convw_in, 16)
            for k, v in enumerate((bf, gf, betaf, mf, vf)):
                sync.dma_start(rows4[k:k + 1, :, :], four(v)).then_inc(rows_in, 16)
            for k, v in ((R_BK, bk), (R_BQ, bq)):
                sync.dma_start(rows[k:k + 1, :], row(v)).then_inc(rows_in, 16)
            sync.dma_start(rows4[R_BH:R_BH + 1, :, :], four(bh)).then_inc(rows_in, 16)
            sync.dma_start(xT[:, 2, :], x_v[:, 2, :]).then_inc(x_in[2], 16)
            for e in range(E):
                sync.dma_start(W1f[:, e, :], W1[e, :, :]).then_inc(w1_in[e], 16)
                sync.dma_start(W2f[:, e, :].rearrange("p (c d) -> p c d", c=FC),
                               W2[e, :, :].rearrange("(c p) d -> p c d", p=P)).then_inc(w2_in[e], 16)
            for g in range(NG):
                sync.wait_ge(acc_added, SUMS - NG + g + 1)
                sync.dma_start(out_v[:, g * GB:(g + 1) * GB, :],
                               acc[:, g * GB:(g + 1) * GB, :]).then_inc(out_stored, 16)
            sync.wait_ge(out_stored, 16 * NG)

        ROWS_IN = 16 * NP
        CONVW_IN = 16 * 5
        ATTNW_IN = 16 * 5

        @block.gpsimd
        def _(pool):
            pool.memset(ident[:, :], 0.0).then_inc(zero_set, 1)
            pool.memset(identb[:, :], 0.0).then_inc(zero_set, 1)
            pool.memset(maskb[:, :], 0.0).then_inc(zero_set, 1)
            pool.memset(sel[:, :, :], 0.0).then_inc(zero_set, 1)
            pool.memset(gateh[:, :, :], 0.0).then_inc(gate_zeroed, 1)
            pool.memset(gatel[:, :, :], 0.0).then_inc(gate_zeroed, 1)
            pool.memset(ones[:, :], 1.0).then_inc(ones_set, 1)
            pool.memset(power[:, :], -0.5).then_inc(consts_set, 1)
            pool.memset(qscale[:, 0:1], float(MID) ** -0.5).then_inc(consts_set, 1)
            pool.memset(qscale[:, 1:2], 1.0).then_inc(consts_set, 1)
            pool.wait_ge(zero_set, 4)
            for m in (ident, identb):
                pool.affine_select(out=m[:, :], in_=m[:, :], compare_op=ALU.not_equal, fill=1.0,
                                   base=0, pattern=[[-1, P]], channel_multiplier=1).then_inc(ident_set, 1)
            pool.affine_select(out=maskb[:, :], in_=maskb[:, :], compare_op=ALU.is_ge, fill=NEG,
                               base=0, pattern=[[1, P]], channel_multiplier=-1).then_inc(mask_set, 1)
            pool.affine_select(out=sel[:, :, :], in_=sel[:, :, :], compare_op=ALU.not_equal, fill=1.0,
                               base=0, pattern=[[-1, E], [0, P]], channel_multiplier=1).then_inc(sel_set, 1)
            pool.iota(iota_e[:, :], pattern=[[1, E]], base=0, channel_multiplier=0,
                      allow_small_or_imprecise_dtypes=True).then_inc(sel_set, 1)
            par = cols[:, 0:10].rearrange("p (w k) -> p w k", k=5)
            pool.wait_ge(setup_copied, 1)
            pool.wait_ge(consts_set, 3)
            pool.tensor_scalar(bn_var[:, :], par[:, :, 4], BN_EPS, None, ALU.add).then_inc(bn_v, 1)
            pool.wait_ge(bn_v, 1)
            pool.tensor_tensor(bn_inv[:, :], bn_var[:, :], power[:, 0:2], ALU.pow).then_inc(bn_v, 1)

            def rstd(mv, ve, rs, mv_ready, ve_ready, rs_ready):
                for b in range(B):
                    i = A * b
                    pool.wait_ge(mv_ready, b + 1)
                    pool.tensor_scalar(ve[:, i:i + A], mv[:, i:i + A, 1], LN_EPS, None,
                                       ALU.add).then_inc(ve_ready, 1)
                    pool.wait_ge(ve_ready, b + 1)
                    pool.tensor_tensor(rs[:, i:i + A], ve[:, i:i + A], power[:, 0:A],
                                       ALU.pow).then_inc(rs_ready, 1)

            rstd(mv0, ve0, rstd0, mv0_ready, ve0_ready, rstd0_ready)
            for b in range(B):
                i = A * b
                pool.wait_ge(y_ready, b + 1)
                pool.tensor_tensor(ty[:, i:i + A, :], t0[:, i:i + A, :], y[:, i:i + A, :],
                                   ALU.add).then_inc(ty_ready, 1)
            rstd(mv1, ve1, rstd1, mv1_ready, ve1_ready, rstd1_ready)
            for b in range(B):
                pool.wait_ge(zT_ready, b + 1)
                pool.tensor_scalar(zh[:, b, :], zT[:, b, :], XS, None, ALU.mult).then_inc(zh_ready, 1)

            def steps(e, first, last):
                for k in range(0, U, 2):
                    n = e * U + k
                    pool.wait_ge(hidh_ready, n + 1)
                    if not (first and k < HB):
                        pool.wait_ge(down_done, n - HB + 1)
                    pool.tensor_tensor(hidl[:, k % HB, :], hid[:, k % HB, :], hidh[:, k % HB, :],
                                       ALU.subtract).then_inc(hidl_even, 1)

            per_expert(pool, steps, lambda: None)

        @block.scalar
        def _(act):
            act.dma_start(xT[:, 1, :], x_v[:, 1, :]).then_inc(x_in[1], 16)
            act.dma_start(wv_s[:, :], wv).then_inc(convw_in, 16)
            act.dma_start(wh_s[:, :], wh).then_inc(convw_in, 16)
            act.dma_start(bv_row[:, :], row(bv)).then_inc(convw_in, 16)
            for k, v in enumerate((bg, gg, betag, mg, vg)):
                act.dma_start(rows4[5 + k:6 + k, :, :], four(v)).then_inc(rows_in, 16)
            act.dma_start(xT[:, 3, :], x_v[:, 3, :]).then_inc(x_in[3], 16)
            act.dma_start(Wk_s[:, :], Wk).then_inc(attnw_in, 16)
            act.dma_start(Wq_s[:, :], Wq).then_inc(attnw_in, 16)
            act.dma_start(Wv_s[:, :], Wv).then_inc(attnw_in, 16)
            act.dma_start(bvalue_row[:, :], row(bvalue)).then_inc(attnw_in, 16)
            act.dma_start(Wgate_s[:, :], Wgate).then_inc(attnw_in, 16)

            act.wait_ge(fg_done, 1)
            act.wait_ge(bn_ready, 1)
            for w in range(2):
                act.activation(fg[:, w, :], pFG[:, w * N:(w + 1) * N], ACT.Relu,
                               bias=bn_bias[:, w:w + 1], scale=bn_scale[:, w:w + 1]).then_inc(fg_ready, 1)
            for b in range(B):
                act.wait_ge(nmax0_ready, b + 1)
                for a in range(A):
                    i = A * b + a
                    act.activation(prob0[:, i, :], pS[b][:, a * N:(a + 1) * N], ACT.Exp,
                                   bias=nmax0[:, i:i + 1], accum_out=sum0[:, i:i + 1]).then_inc(prob0_ready, 1)
            for b in range(B):
                act.wait_ge(pT_done, b + 1)
                act.activation(prob0T[:, A * b:A * b + A, :].rearrange("p a n -> p (a n)"),
                               pPT[b][:, :], ACT.Copy).then_inc(prob0T_ready, 1)
            for b in range(B):
                act.wait_ge(kq_done, b + 1)
                act.activation(kT[:, b, :], pKQ[b][:, 0:N], ACT.Identity,
                               bias=cols[:, R_BK:R_BK + 1]).then_inc(kq_ready, 1)
                act.activation(qT[:, b, :], pKQ[b][:, N:2 * N], ACT.Identity,
                               bias=cols[:, R_BQ:R_BQ + 1]).then_inc(kq_ready, 1)
            for b in range(B):
                act.wait_ge(nmax1_ready, A * (b + 1))
                for a in range(A):
                    i = A * b + a
                    lo, hi = (0, N) if a == 0 else (N, LW)
                    act.activation(prob1[:, b, lo:hi], pL[b][:, lo:hi], ACT.Exp,
                                   bias=nmax1[:, i:i + 1], accum_out=sum1[:, i:i + 1]).then_inc(prob1_ready, 1)
            for b in range(B):
                act.wait_ge(zT_done, b + 1)
                act.activation(zT[:, b, :], pZ[b][:, 0:N], ACT.Copy).then_inc(zT_ready, 1)
                act.activation(acc[:, b, :], pZ[b][:, N:2 * N], ACT.Copy).then_inc(acc_ready, 1)

            def high_parts(e):
                act.activation(W1h[:, e, :], W1f[:, e, :], ACT.Copy, scale=WS).then_inc(wh_ready, 1)
                act.activation(W2h[:, e, :], W2f[:, e, :], ACT.Copy, scale=WS).then_inc(wh_ready, 1)

            for e in range(E):
                act.wait_ge(w1_in[e], 16)
                act.wait_ge(w2_in[e], 16)
            high_parts(0)
            for g in range(NG):
                act.wait_ge(gap_ready, g + 1)
                act.activation(e2[:, g * GT:(g + 1) * GT, :], gap[:, g * GT:(g + 1) * GT, :],
                               ACT.Exp).then_inc(e2_ready, 1)
            act.wait_ge(gate_zeroed, 2)
            for g in range(NG):
                act.wait_ge(gateT_done, g + 1)
                act.activation(gateh[0:E, g, :], pCT[g][0:E, :], ACT.Copy).then_inc(gateh_ready, 1)

            def steps(e, first, last):
                for k in range(U):
                    n = e * U + k
                    act.wait_ge(up_done, n + 1)
                    if not (first and k < HB):
                        act.wait_ge(hidl_odd if k % 2 else hidl_even, e * (U // 2) + k // 2 - HB // 2 + 1)
                    act.activation(hid[:, k % HB, :], pUP[k % HB][:, :], ACT.Silu,
                                   scale=1.0 / (XS * WS)).then_inc(hid_ready, 1)
                    if k % FC == 0:
                        d = e * NG + k // FC
                        act.wait_ge(gw_done, d + 1)
                        if not first:
                            act.wait_ge(gated_ready, d - 1)
                        act.activation(gatew[:, (k // FC) % 2, :], pGW[(k // FC) % 2][:, :], ACT.Copy,
                                       scale=1.0 / (CS * WS)).then_inc(gatew_ready, 1)
                    if k == 1 and not last:
                        act.activation(W1h[:, e + 1, :], W1f[:, e + 1, :], ACT.Copy,
                                       scale=WS).then_inc(wh_ready, 1)
                    if k == 3 and not last:
                        act.activation(W2h[:, e + 1, :], W2f[:, e + 1, :], ACT.Copy,
                                       scale=WS).then_inc(wh_ready, 1)

            per_expert(act, steps, lambda: None)

        @block.vector
        def _(dve):
            dve.wait_ge(setup_T, 1)
            dve.tensor_copy(cols[:, :], pSET[:, 256:256 + NP]).then_inc(setup_copied, 1)
            dve.tensor_copy(wfT[:, :], pSET[:, 0:2 * MID]).then_inc(setup_copied, 1)
            dve.tensor_copy(wvT[:, :], pSET[0:MID, P:2 * P]).then_inc(setup_copied, 1)
            dve.wait_ge(setup_copied, 3)
            dve.wait_ge(ones_set, 1)
            dve.tensor_scalar(bh_wide[:, :], ones[0:MID, :], cols[0:MID, R_BH:R_BH + 1], None,
                              ALU.mult).then_inc(bh_widened, 1)
            par = cols[:, 0:10].rearrange("p (w k) -> p w k", k=5)
            dve.wait_ge(bn_v, 2)
            dve.tensor_tensor(bn_inv[:, :], bn_inv[:, :], par[:, :, 1], ALU.mult).then_inc(bn_v, 1)
            dve.tensor_tensor(bn_tmp[:, :], par[:, :, 0], par[:, :, 3], ALU.subtract).then_inc(bn_v, 1)
            dve.tensor_tensor(bn_beta[:, :], par[:, :, 2], qscale[:, :], ALU.mult).then_inc(bn_v, 1)
            dve.wait_ge(bn_v, 5)
            dve.tensor_tensor(bn_scale[:, :], bn_inv[:, :], qscale[:, :], ALU.mult).then_inc(bn_v, 1)
            dve.wait_ge(bn_v, 6)
            dve.tensor_tensor(bn_tmp[:, :], bn_tmp[:, :], bn_scale[:, :], ALU.mult).then_inc(bn_v, 1)
            dve.wait_ge(bn_v, 7)
            dve.tensor_tensor(bn_bias[:, :], bn_tmp[:, :], bn_beta[:, :], ALU.add).then_inc(bn_ready, 1)
            dve.wait_ge(fold_done, 1)
            dve.tensor_copy(fold[:, :, :].rearrange("p k n -> p (k n)"), pFOLD[:, 0:3 * P]).then_inc(fold_copied, 1)
            dve.wait_ge(fold_copied, 1)
            for g in range(NG):
                dve.wait_ge(xT_done, g + 1)
                dve.tensor_tensor(xb[:, g * GT:(g + 1) * GT, :],
                                  pX[g][:, :].rearrange("p (t n) -> p t n", n=P),
                                  fold[:, 1:2, :].broadcast_to([P, GT, P]), ALU.add).then_inc(xb_ready, 1)
            for g in range(NG):
                dve.wait_ge(hv_done, g + 1)
                dve.tensor_copy(hv[:, g * GT:(g + 1) * GT, :].rearrange("p t n -> p (t n)"),
                                pHV[g][:, :]).then_inc(hv_ready, 1)
            for b in range(B):
                dve.wait_ge(s_done, b + 1)
                dve.tensor_reduce(nmax0[:, A * b:A * b + A], pS[b][:, :].rearrange("p (a n) -> p a n", a=A),
                                  AX.X, ALU.max, negate=True).then_inc(nmax0_ready, 1)
            for b in range(B):
                dve.wait_ge(prob0_ready, A * (b + 1))
                dve.reciprocal(rec0[:, A * b:A * b + A], sum0[:, A * b:A * b + A]).then_inc(rec0_ready, 1)
            for b in range(B):
                dve.wait_ge(u_done, b + 1)
                dve.wait_ge(rec0_ready, b + 1)
                dve.wait_ge(xb_ready, b // GB + 1)
                for a in range(A):
                    i = A * b + a
                    dve.scalar_tensor_tensor(out=t0[:, i, :], in0=pU[b][:, a * P:(a + 1) * P],
                                             scalar=rec0[:, i:i + 1], in1=xb[:, i, :],
                                             op0=ALU.mult, op1=ALU.add).then_inc(t0_ready, 1)

            def layer_norm(src, st, mv, rs, dst, src_ready, src_per, st_ready, mv_ready, rs_ready, dst_ready):
                for b in range(B):
                    dve.wait_ge(src_ready, src_per * (b + 1))
                    for i in range(A * b, A * b + A):
                        dve.bn_stats(st[:, i, :], src[:, i, :]).then_inc(st_ready, 1)
                for b in range(B):
                    dve.wait_ge(st_ready, A * (b + 1))
                    for i in range(A * b, A * b + A):
                        last = dve.bn_aggr(mv[:, i, :], st[:, i, :])
                    last.then_inc(mv_ready, 1)
                for b in range(B):
                    dve.wait_ge(mv_ready, b + 1)
                    dve.wait_ge(rs_ready, b + 1)
                    for i in range(A * b, A * b + A):
                        last = dve.tensor_scalar(dst[:, i, :], src[:, i, :], mv[:, i, 0:1], rs[:, i:i + 1],
                                                 ALU.subtract, ALU.mult)
                    last.then_inc(dst_ready, 1)

            layer_norm(t0, st0, mv0, rstd0, y, t0_ready, A, st0_ready, mv0_ready, rstd0_ready, y_ready)
            for b in range(B):
                dve.wait_ge(yT_done, b + 1)
                dve.tensor_copy(yT[:, b, :], pYT[b][:, 0:N]).then_inc(yT_ready, 1)
            for b in range(B):
                dve.wait_ge(v_done, b + 1)
                dve.tensor_tensor(val[:, A * b:A * b + A, :],
                                  pV[b][:, 0:A * P].rearrange("p (a n) -> p a n", a=A),
                                  fold[:, 2:3, :].broadcast_to([P, A, P]), ALU.add).then_inc(val_ready, 1)
            for b in range(B):
                dve.wait_ge(l_done, b + 1)
                for a in range(A):
                    i = A * b + a
                    lo, hi = (0, N) if a == 0 else (N, LW)
                    dve.tensor_reduce(nmax1[:, i:i + 1], pL[b][:, lo:hi], AX.X, ALU.max,
                                      negate=True).then_inc(nmax1_ready, 1)
            for b in range(B):
                dve.wait_ge(prob1_ready, A * (b + 1))
                dve.reciprocal(rec1[:, A * b:A * b + A], sum1[:, A * b:A * b + A]).then_inc(rec1_ready, 1)
            for b in range(B):
                dve.wait_ge(rec1_ready, b + 1)
                dve.wait_ge(val_ready, b + 1)
                for i in range(A * b, A * b + A):
                    last = dve.tensor_scalar(vals[:, i, :], val[:, i, :], rec1[:, i:i + 1],
                                             float(P) ** -0.5, ALU.mult, ALU.mult)
                last.then_inc(vals_ready, 1)
            for b in range(B):
                dve.wait_ge(r_done, b + 1)
                dve.wait_ge(ty_ready, b + 1)
                dve.tensor_tensor(t1[:, A * b:A * b + A, :].rearrange("p a n -> p (a n)"),
                                  pR[b][:, 0:A * P],
                                  ty[:, A * b:A * b + A, :].rearrange("p a n -> p (a n)"),
                                  ALU.add).then_inc(t1_ready, 1)
            layer_norm(t1, st1, mv1, rstd1, z, t1_ready, 1, st1_ready, mv1_ready, rstd1_ready, z_ready)

            for g in range(NG):
                r = slice(g * GT, (g + 1) * GT)
                dve.wait_ge(rt_done, g + 1)
                dve.tensor_copy(rl[:, r, :].rearrange("p t e -> p (t e)"), pRT[g][:, 0:GT * E]).then_inc(rl_ready, 1)
                dve.wait_ge(rl_ready, g + 1)
                for i in range(g * GT, (g + 1) * GT):
                    dve.max(top[:, i, :], rl[:, i, :]).then_inc(top_ready, 1)
                dve.wait_ge(top_ready, (g + 1) * GT)
                dve.tensor_tensor(gap[:, r, :], top[:, r, 1:2], top[:, r, 0:1], ALU.subtract).then_inc(gap_ready, 1)
                for i in range(g * GT, (g + 1) * GT):
                    dve.max_index(topi[:, i, :], top[:, i, :], rl[:, i, :]).then_inc(topi_ready, 1)
                dve.wait_ge(topi_ready, (g + 1) * GT)
                dve.tensor_copy(topf[:, r, :], topi[:, r, 0:2]).then_inc(topf_ready, 1)
                dve.wait_ge(topf_ready, g + 1)
                dve.wait_ge(sel_set, 2)
                lane = iota_e[:, :].unsqueeze(1).broadcast_to([P, GT, E])
                dve.tensor_tensor(oh1[:, r, :], topf[:, r, 0:1].broadcast_to([P, GT, E]), lane,
                                  ALU.is_equal).then_inc(oh_ready, 1)
                dve.tensor_tensor(oh2[:, r, :], topf[:, r, 1:2].broadcast_to([P, GT, E]), lane,
                                  ALU.is_equal).then_inc(oh_ready, 1)
                dve.wait_ge(e2_ready, g + 1)
                dve.tensor_scalar(den[:, r, :], e2[:, r, :], 1.0, 1.0 / CS, ALU.add, ALU.mult).then_inc(den_ready, 1)
                dve.wait_ge(den_ready, g + 1)
                dve.reciprocal(g1[:, r, :], den[:, r, :]).then_inc(g1_ready, 1)
                dve.wait_ge(g1_ready, g + 1)
                dve.tensor_tensor(g2[:, r, :], g1[:, r, :], e2[:, r, :], ALU.mult).then_inc(g2_ready, 1)
                dve.wait_ge(oh_ready, 2 * (g + 1))
                dve.tensor_tensor(gw1[:, r, :], oh1[:, r, :], g1[:, r, :].broadcast_to([P, GT, E]),
                                  ALU.mult).then_inc(gw_ready, 1)
                dve.wait_ge(g2_ready, g + 1)
                dve.tensor_tensor(gw2[:, r, :], oh2[:, r, :], g2[:, r, :].broadcast_to([P, GT, E]),
                                  ALU.mult).then_inc(gw_ready, 1)
                dve.wait_ge(gw_ready, 2 * (g + 1))
                dve.tensor_tensor(gate[:, r, :], gw1[:, r, :], gw2[:, r, :], ALU.add).then_inc(gate_ready, 1)
            for b in range(B):
                dve.wait_ge(zh_ready, b + 1)
                dve.scalar_tensor_tensor(out=zl[:, b, :], in0=zT[:, b, :], scalar=XS, in1=zh[:, b, :],
                                         op0=ALU.mult, op1=ALU.subtract).then_inc(zl_ready, 1)
            dve.wait_ge(wh_ready, 1)
            dve.scalar_tensor_tensor(out=W1l[:, 0, :], in0=W1f[:, 0, :], scalar=WS, in1=W1h[:, 0, :],
                                     op0=ALU.mult, op1=ALU.subtract).then_inc(wl_ready, 1)
            dve.wait_ge(wh_ready, 2)
            dve.scalar_tensor_tensor(out=W2l[:, 0, :], in0=W2f[:, 0, :], scalar=WS, in1=W2h[:, 0, :],
                                     op0=ALU.mult, op1=ALU.subtract).then_inc(wl_ready, 1)
            for g in range(NG):
                dve.wait_ge(gateh_ready, g + 1)
                dve.tensor_tensor(gatel[0:E, g, :], pCT[g][0:E, :], gateh[0:E, g, :],
                                  ALU.subtract).then_inc(gatel_ready, 1)

            def gate_sum(d, d2):
                g = d2 % NG
                a = acc[:, g * GB:(g + 1) * GB, :].rearrange("p b n -> p (b n)")
                dve.wait_ge(down_done, (d + 1) * FC)
                dve.wait_ge(gatew_ready, d + 1)
                dve.tensor_tensor(gated[:, d2 % 2, :], pDN[d2 % 2][:, :], gatew[:, d2 % 2, :],
                                  ALU.mult).then_inc(gated_ready, 1)
                if isinstance(d, int) and d == 0:
                    dve.wait_ge(acc_ready, B)
                dve.wait_ge(gated_ready, d + 1)
                dve.tensor_tensor(a, a, gated[:, d2 % 2, :], ALU.add).then_inc(acc_added, 1)

            def steps(e, first, last):
                for k in range(U):
                    n = e * U + k
                    dve.wait_ge(hid_ready, n + 1)
                    if not (first and k < HB):
                        dve.wait_ge(down_done, n - HB + 1)
                    dve.tensor_copy(hidh[:, k % HB, :], hid[:, k % HB, :]).then_inc(hidh_ready, 1)
                    if k % 2:
                        dve.wait_ge(hidh_ready, n + 1)
                        dve.tensor_tensor(hidl[:, k % HB, :], hid[:, k % HB, :], hidh[:, k % HB, :],
                                          ALU.subtract).then_inc(hidl_odd, 1)
                    if k == LAG - 1 and not first:
                        gate_sum(e * NG - 1, NG - 1)
                    if k == LAG - 1 + FC:
                        gate_sum(e * NG, 0)
                    if k == 3 and not last:
                        dve.wait_ge(wh_ready, 2 * e + 3)
                        dve.scalar_tensor_tensor(out=W1l[:, e + 1, :], in0=W1f[:, e + 1, :], scalar=WS,
                                                 in1=W1h[:, e + 1, :], op0=ALU.mult,
                                                 op1=ALU.subtract).then_inc(wl_ready, 1)
                    if k == 5 and not last:
                        dve.wait_ge(wh_ready, 2 * e + 4)
                        dve.scalar_tensor_tensor(out=W2l[:, e + 1, :], in0=W2f[:, e + 1, :], scalar=WS,
                                                 in1=W2h[:, e + 1, :], op0=ALU.mult,
                                                 op1=ALU.subtract).then_inc(wl_ready, 1)

            per_expert(dve, steps, lambda: gate_sum(SUMS - 1, SUMS - 1))

        @block.tensor
        def _(pe):
            pe.wait_ge(ident_set, 2)
            pe.wait_ge(convw_in, CONVW_IN)
            pe.transpose(pSET[:, 0:MID], wf_s[:, :], ident[0:MID, 0:MID])
            pe.transpose(pSET[:, MID:2 * MID], wg_s[:, :], ident[0:MID, 0:MID])
            pe.transpose(pSET[0:MID, P:2 * P], wv_s[:, :], ident[:, :])
            pe.wait_ge(rows_in, ROWS_IN)
            pe.transpose(pSET[:, 256:256 + NP], rows[:, :], ident[0:NP, 0:NP]).then_inc(setup_T, 1)
            for g in range(NG):
                for b in range(g * GB, (g + 1) * GB):
                    pe.wait_ge(x_in[b], 16)
                    for a in range(A):
                        col = (A * b + a - g * GT) * P
                        last = pe.transpose(pX[g][:, col:col + P], xT[:, b, a * P:(a + 1) * P], ident[:, :])
                last.then_inc(xT_done, 1)
            pe.wait_ge(setup_copied, 3)
            for w in range(2):
                for b in range(B):
                    last = pe.matmul(pFG[b * MID:(b + 1) * MID, w * N:(w + 1) * N],
                                     wfT[:, w * MID:(w + 1) * MID], xT[:, b, :], start=True, stop=True)
            last.then_inc(fg_done, 1)
            pe.matmul(pFOLD[:, 0:P], wh_s[:, :], wvT[:, :], start=True, stop=True)
            pe.wait_ge(bh_widened, 1)
            pe.matmul(pFOLD[:, P:2 * P], bh_wide[:, :], wvT[:, :], start=True, stop=False)
            pe.matmul(pFOLD[:, P:2 * P], ones[0:1, :], bv_row[:, :], start=False, stop=True)
            pe.wait_ge(attnw_in, ATTNW_IN)
            pe.matmul(pFOLD[:, 2 * P:3 * P], ones[0:1, :], bvalue_row[:, :], start=True,
                      stop=True).then_inc(fold_done, 1)
            pe.wait_ge(fold_copied, 1)
            for g in range(NG):
                for i in range(g * GT, (g + 1) * GT):
                    col = (i - g * GT) * P
                    last = pe.matmul(pHV[g][:, col:col + P], xT[:, i // A, (i % A) * P:(i % A + 1) * P],
                                     fold[:, 0, :], start=True, stop=True)
                last.then_inc(hv_done, 1)
            pe.wait_ge(fg_ready, 2)
            for b in range(B):
                r = slice(b * MID, (b + 1) * MID)
                for a in range(A):
                    last = pe.matmul(pS[b][:, a * N:(a + 1) * N], fg[r, 0, a * P:(a + 1) * P],
                                     fg[r, 1, :], start=True, stop=True)
                last.then_inc(s_done, 1)
            pe.wait_ge(hv_ready, NG)
            pe.wait_ge(xb_ready, NG)
            for b in range(B):
                pe.wait_ge(prob0_ready, A * (b + 1))
                for j in range(A):
                    for a in range(A):
                        col = j * N + a * P
                        last = pe.transpose(pPT[b][:, col:col + P],
                                            prob0[:, A * b + a, j * P:(j + 1) * P], ident[:, :])
                last.then_inc(pT_done, 1)
            for b in range(B):
                pe.wait_ge(prob0T_ready, b + 1)
                for a in range(A):
                    for j in range(A):
                        last = pe.matmul(pU[b][:, a * P:(a + 1) * P],
                                         prob0T[:, A * b + j, a * P:(a + 1) * P], hv[:, A * b + j, :],
                                         start=(j == 0), stop=(j == A - 1))
                last.then_inc(u_done, 1)
            for b in range(B):
                pe.wait_ge(y_ready, b + 1)
                for a in range(A):
                    last = pe.transpose(pYT[b][:, a * P:(a + 1) * P], y[:, A * b + a, :], ident[:, :])
                last.then_inc(yT_done, 1)
            for b in range(B):
                pe.wait_ge(yT_ready, b + 1)
                pe.matmul(pKQ[b][:, 0:N], Wk_s[:, :], yT[:, b, :], start=True, stop=True)
                pe.matmul(pKQ[b][:, N:2 * N], Wq_s[:, :], yT[:, b, :], start=True,
                          stop=True).then_inc(kq_done, 1)
                for a in range(A):
                    last = pe.matmul(pV[b][:, a * P:(a + 1) * P], yT[:, b, a * P:(a + 1) * P],
                                     Wv_s[:, :], start=True, stop=True)
                last.then_inc(v_done, 1)
            pe.wait_ge(mask_set, 1)
            for b in range(B):
                pe.wait_ge(kq_ready, 2 * (b + 1))
                for a in range(A):
                    lo, hi = (0, N) if a == 0 else (N, LW)
                    pe.matmul(pL[b][:, lo:hi], kT[:, b, a * P:(a + 1) * P], qT[:, b, a * P:N],
                              start=True, stop=False)
                    last = pe.matmul(pL[b][:, lo:lo + P], identb[:, :], maskb[:, :],
                                     start=False, stop=True)
                last.then_inc(l_done, 1)
            for b in range(B):
                pe.wait_ge(prob1_ready, A * (b + 1))
                pe.wait_ge(vals_ready, b + 1)
                pe.matmul(pR[b][:, 0:P], prob1[:, b, 0:P], vals[:, A * b, :], start=True, stop=True)
                pe.matmul(pR[b][:, P:2 * P], prob1[:, b, P:N], vals[:, A * b, :], start=True, stop=False)
                pe.matmul(pR[b][:, P:2 * P], prob1[:, b, N:LW], vals[:, A * b + 1, :], start=False,
                          stop=True).then_inc(r_done, 1)
            for b in range(B):
                pe.wait_ge(z_ready, b + 1)
                for a in range(A):
                    i = A * b + a
                    pe.transpose(pZ[b][:, a * P:(a + 1) * P], z[:, i, :], ident[:, :])
                    last = pe.transpose(pZ[b][:, N + a * P:N + (a + 1) * P], t1[:, i, :], ident[:, :])
                last.then_inc(zT_done, 1)
            for g in range(NG):
                for b in range(g * GB, (g + 1) * GB):
                    pe.wait_ge(zT_ready, b + 1)
                    for a in range(A):
                        col = (A * b + a - g * GT) * E
                        last = pe.matmul(pRT[g][:, col:col + E], zT[:, b, a * P:(a + 1) * P],
                                         Wgate_s[:, :], start=True, stop=True)
                last.then_inc(rt_done, 1)
            for g in range(NG):
                pe.wait_ge(gate_ready, g + 1)
                for i in range(g * GT, (g + 1) * GT):
                    col = (i - g * GT) * P
                    last = pe.transpose(pCT[g][0:E, col:col + P], gate[:, i, :], ident[:, :])
                last.then_inc(gateT_done, 1)

            pe.wait_ge(sel_set, 1)
            pe.wait_ge(zl_ready, B)
            pe.wait_ge(zh_ready, B)
            pe.wait_ge(acc_ready, B)
            pe.wait_ge(gatel_ready, NG)

            def down(m, e, k):
                pe.wait_ge(hidl_odd if k % 2 else hidl_even, e * (U // 2) + k // 2 + 1)
                if k % FC == 0 and not (isinstance(m, int) and m < 2 * FC):
                    pe.wait_ge(gated_ready, e * NG + k // FC - 1)
                ch = slice((k % FC) * P, (k % FC + 1) * P)
                o = pDN[(k // FC) % 2][:, :]
                pe.matmul(o, W2h[:, e, ch], hidh[:, k % HB, :], start=(k % FC == 0), stop=False)
                pe.matmul(o, W2h[:, e, ch], hidl[:, k % HB, :], start=False, stop=False)
                pe.matmul(o, W2l[:, e, ch], hidh[:, k % HB, :], start=False,
                          stop=(k % FC == FC - 1)).then_inc(down_done, 1)

            def steps(e, first, last):
                pe.wait_ge(wl_ready, 2 * e + 2)
                pe.wait_ge(wh_ready, 2 * e + 2)
                for k in range(U):
                    n = e * U + k
                    g = k // FC
                    if k % FC == 0:
                        if not first:
                            pe.wait_ge(gatew_ready, e * NG + g - 1)
                        pe.matmul(pGW[g % 2][:, :], sel[:, e, :], gateh[:, g, :], start=True, stop=False)
                        pe.matmul(pGW[g % 2][:, :], sel[:, e, :], gatel[:, g, :], start=False,
                                  stop=True).then_inc(gw_done, 1)
                    if not (first and k < HB):
                        pe.wait_ge(hid_ready, n - HB + 1)
                    ch = slice((k % FC) * P, (k % FC + 1) * P)
                    th = zh[:, g * GB:(g + 1) * GB, :].rearrange("p b n -> p (b n)")
                    tl = zl[:, g * GB:(g + 1) * GB, :].rearrange("p b n -> p (b n)")
                    o = pUP[k % HB][:, :]
                    pe.matmul(o, W1h[:, e, ch], th, start=True, stop=False)
                    pe.matmul(o, W1h[:, e, ch], tl, start=False, stop=False)
                    pe.matmul(o, W1l[:, e, ch], th, start=False, stop=True).then_inc(up_done, 1)
                    if k >= LAG:
                        down(n - LAG, e, k - LAG)
                    elif not first:
                        down(n - LAG, e - 1, k - LAG + U)

            def tail():
                for m in range(UNITS - LAG, UNITS):
                    down(m, E - 1, m % U)

            per_expert(pe, steps, tail)


_INS = ['x', 'L0_conv_wf', 'L0_conv_bf', 'L0_conv_gf', 'L0_conv_betaf', 'L0_conv_mf', 'L0_conv_vf',
        'L0_conv_wg', 'L0_conv_bg', 'L0_conv_gg', 'L0_conv_betag', 'L0_conv_mg', 'L0_conv_vg',
        'L0_conv_wh', 'L0_conv_bh', 'L0_conv_wv', 'L0_conv_bv',
        'L1_attn_Wk', 'L1_attn_bk', 'L1_attn_Wq', 'L1_attn_bq', 'L1_attn_Wv', 'L1_attn_bv',
        'L1_ffn_Wg', 'L1_ffn_W1', 'L1_ffn_W2']
_OUTS = [((4, 128, 16, 16), 'float32')]


def kernel(**inputs):
    import numpy as _np
    import concourse.bacc as _bacc
    from concourse import mybir as _mybir
    from concourse.bass_utils import run_bass_kernel_spmd as _run

    nc = _bacc.Bacc("TRN2", target_bir_lowering=False, num_devices=1)
    arrays, args = {}, []
    for name in _INS:
        a = _np.ascontiguousarray(inputs[name])
        arrays[f"in_{name}_dram"] = a
        args.append(nc.dram_tensor(f"in_{name}_dram", a.shape, _mybir.dt.from_np(a.dtype), kind="ExternalInput").ap())
    for i, (shape, dtype) in enumerate(_OUTS):
        dt = _mybir.dt.from_np(_np.dtype(dtype))
        args.append(nc.dram_tensor(f"out_{i}_dram", shape, dt, kind="ExternalOutput").ap())
    conv_attention_moe_kernel(nc, *args)
    r = _run(nc, [arrays], core_ids=[0])
    got = tuple(r.results[0][f"out_{i}_dram"] for i in range(len(_OUTS)))
    return got[0]
```

```python
import concourse.bass as bass
from concourse import mybir
from contextlib import ExitStack


def conv_attention_moe_kernel(
    nc: bass.Bass,
    x: bass.AP,
    wf: bass.AP, bf: bass.AP, gf: bass.AP, betaf: bass.AP, mf: bass.AP, vf: bass.AP,
    wg: bass.AP, bg: bass.AP, gg: bass.AP, betag: bass.AP, mg: bass.AP, vg: bass.AP,
    wh: bass.AP, bh: bass.AP, wv: bass.AP, bv: bass.AP,
    Wk: bass.AP, bk: bass.AP, Wq: bass.AP, bq: bass.AP, Wv: bass.AP, bvalue: bass.AP,
    Wgate: bass.AP, W1: bass.AP, W2: bass.AP,
    out: bass.AP,
):
    fp32 = mybir.dt.float32
    fp16 = mybir.dt.float16
    bf16 = mybir.dt.bfloat16
    u32 = mybir.dt.uint32
    ALU = mybir.AluOpType
    ACT = mybir.ActivationFunctionType
    AX = mybir.AxisListType

    B, C, H, W = x.shape
    N = H * W
    P = 128
    A = N // P
    T = B * A
    MID = wf.shape[0]
    E, _, F = W1.shape
    FC = F // P
    NH = 2
    HBT = B // NH
    HT = T // NH
    HN = HT * P
    TOPS = 8
    BN_EPS = 1e-5
    LN_EPS = 1e-5
    NEG = -1e30
    XS = 16.0
    WS = 256.0

    x_v = x.rearrange("b c h w -> c b (h w)")
    out_v = out.rearrange("b c h w -> c b (h w)")
    gates_dram = nc.dram_tensor("gates_dram", [NH, E, HN], fp32).ap()

    def row(v, n=1):
        return v.rearrange("(a n) -> a n", a=n)

    def per_batch(v):
        return row(v).unsqueeze(1).broadcast_to([1, B, MID])

    def half(h):
        return slice(h * HBT, (h + 1) * HBT)

    UNITS = NH * E * FC
    SUMS = NH * E
    LAG = 3
    HB = 4
    POOL_LOW = ((0, 1, 2), (0, 2))
    ACT_HIGH = ((), ())

    PLAN = {
        "tokens_split": (-23.00, 11.13),
        "bn_pow": (-15.11,),
        "convsT": (-12.36,),
        "tokens": (-4.98, 20.57),
        "convs_copy": (-3.70,),
        "tokens_high": (-2.72, 0.54),
        "branches_low": (-1.55, 4.54, 8.28, 18.57),
        "bnT": (-1.33,),
        "relus": (2.26, 7.84, 14.48, 22.90),
        "convs": (5.48, 6.07, 10.46, 19.20),
        "bn_copy": (6.04,),
        "foldT": (7.09,),
        "bn_fold": (9.92,),
        "fold": (11.77,),
        "scores": (11.94, 14.51, 20.24, 21.61),
        "attention_high": (12.24,),
        "branch": (13.62, 19.30),
        "branches_high": (15.33, 16.35, 17.60, 19.03),
        "fold_prepare": (15.88,),
        "fold_copy": (16.93,),
        "tokens_copy": (17.15, 19.67),
        "max0": (17.37, 18.87, 19.47, 23.04),
        "rec0": (18.99, 23.17, 28.12, 31.24),
        "probsT": (19.70, 21.57, 22.81, 23.54),
        "mix": (21.34, 22.47, 23.65, 24.57),
        "rstd0": (21.42, 22.11, 27.69, 27.96),
        "add0": (21.55, 27.89, 32.00, 33.60),
        "stats0": (21.99, 29.54, 33.05, 34.52),
        "branch_copy": (22.35, 24.72),
        "exp0": (22.70, 23.34, 26.21, 26.51),
        "probsT_copy": (23.13, 25.94, 28.11, 28.58),
        "residual": (23.22, 27.53, 37.80, 52.11),
        "normT": (24.55, 28.29, 30.44, 31.63),
        "aggr0": (25.51, 31.20, 33.94, 35.70),
        "keys": (26.26, 29.24, 35.69, 38.71),
        "attention_low": (26.51,),
        "norm0": (28.85, 33.25, 36.20, 36.35),
        "values": (28.88, 32.75, 36.87, 43.30),
        "logits": (29.04, 36.44, 38.56, 43.91),
        "norm_high": (29.57, 33.01, 33.17, 33.81),
        "normT_copy": (32.23, 34.93, 36.58, 37.60),
        "keys_copy": (32.47, 33.46, 35.24, 42.74),
        "weights": (33.13, 51.98, 52.90, 70.65, 71.05, 75.16, 84.90, 89.27),
        "exp1": (34.60, 42.32, 44.02, 48.00),
        "values_copy": (36.22, 37.28, 39.21, 44.25),
        "max1": (36.65, 38.68, 42.66, 45.81),
        "rstd1": (37.42, 44.61, 52.36, 53.50),
        "read": (38.19, 43.29, 46.17, 50.47),
        "rec1": (38.22, 39.53, 45.10, 47.75),
        "scale_values": (38.34, 41.15, 45.98, 48.30),
        "add1": (39.37, 43.47, 46.95, 48.85),
        "stats1": (42.18, 44.36, 47.63, 50.03),
        "aggr1": (43.06, 45.28, 47.95, 50.78),
        "norm1": (45.64, 46.18, 48.63, 53.39),
        "finalT": (45.90, 48.31, 51.83, 53.11),
        "weights_low": (46.52, 54.71, 63.51, 68.83, 71.22, 79.16, 83.27, 90.02),
        "tokens_low": (47.12, 47.48, 52.92, 54.91),
        "final_copy": (47.76, 49.12, 54.50, 56.62),
        "route_copy": (47.95, 56.65),
        "top_two": (48.48, 58.06),
        "route": (48.75, 56.25),
        "one_hots": (48.86, 61.86),
        "gate_tokens": (51.12, 65.69),
        "tanh": (52.90, 63.56),
        "gatesT": (53.10, 70.57),
        "gatesT_copy": (59.81, 76.28),
    }
    UNIT_TIMES = (
        49.23, 52.98, 53.07, 54.08, 58.46, 60.42, 63.97, 64.40, 66.82, 68.88, 70.17,
        71.29, 72.44, 74.85, 76.59, 77.60, 78.09, 80.13, 82.11, 82.26, 86.63, 94.13,
        97.94, 105.01, 106.48, 107.43, 107.62, 110.55, 120.70, 142.30, 161.57, 161.95)
    WARM = (
        (-1.09, 1), (0.23, 1), (30.75, 1),)
    WARM_UP = 5

    def order(steps, unit_delay):
        at = [(t, step, k) for step, times in PLAN.items() for k, t in enumerate(times)]
        at += [(t + unit_delay, "unit", n) for n, t in enumerate(UNIT_TIMES)]
        at += [(t, "warm", k) for t, k in WARM]
        return [(step, k) for _, step, k in sorted(at) if step in steps]

    ctx = ExitStack()
    with ctx:
        def sb(name, shape, dt=fp32):
            return ctx.enter_context(nc.sbuf_tensor(name, shape, dt))

        def sem(name):
            return ctx.enter_context(nc.semaphore(name))

        xT = sb("xT", [P, B, N])
        bn_rows = sb("bn_rows", [10, P])
        bn_rows4 = bn_rows[:, :].rearrange("p (b m) -> p b m", b=B)
        bn_cols = sb("bn_cols", [P, 10])
        bias_rows = sb("bias_rows", [3, P])
        bias_rows4 = bias_rows[:, :].rearrange("p (b m) -> p b m", b=B)
        bias_cols = sb("bias_cols", [P, 3])
        wf_s = sb("wf_s", [MID, P])
        wg_s = sb("wg_s", [MID, P])
        wh_s = sb("wh_s", [MID, P])
        wv_s = sb("wv_s", [P, MID])
        MK = 3 * MID
        wfgT = sb("wfgT", [P, 2, 3, MID])
        wfgTh = sb("wfgTh", [P, 2, MK], fp16)
        wfgTl = sb("wfgTl", [P, 2, MK], fp16)
        xh = sb("xh", [P, B, N], fp16)
        xl = sb("xl", [P, B, N], fp16)
        wvT = sb("wvT", [MID, P])
        bh_wide = sb("bh_wide", [MID, P])
        bv_row = sb("bv_row", [1, P])
        bvalue_row = sb("bvalue_row", [1, P])
        fold = sb("fold", [P, 3, P])
        foldh = sb("foldh", [P, P], fp16)
        foldl = sb("foldl", [P, P], fp16)
        ident = sb("ident", [P, P])
        identb = sb("identb", [P, P], bf16)
        maskb = sb("maskb", [P, P], bf16)
        warm_b = sb("warm_b", [P, 512], bf16)
        ones = sb("ones", [P, P])
        iota_e = sb("iota_e", [P, E])
        power = sb("power", [P, 2])
        qscale = sb("qscale", [P, 2])
        bn_var = sb("bn_var", [P, 2])
        bn_inv = sb("bn_inv", [P, 2])
        bn_gain = sb("bn_gain", [P, 2])
        bn_scale = sb("bn_scale", [P, 2])
        bn_off = sb("bn_off", [P, 2])
        bn_move = sb("bn_move", [P, 2])
        bn_beta = sb("bn_beta", [P, 2])
        bn_bias = sb("bn_bias", [P, 2])
        bn_scale_w = sb("bn_scale_w", [P, 2])
        fg = sb("fg", [MK, 2, 2, N])
        fg3 = sb("fg3", [MK, B, 2, N], fp16)
        hv = sb("hv", [P, T, P])
        xb = sb("xb", [P, T, P])
        nmax0 = sb("nmax0", [P, T])
        sum0 = sb("sum0", [P, T])
        rec0 = sb("rec0", [P, T])
        prob0 = sb("prob0", [P, T, N])
        prob0T = sb("prob0T", [P, T, N])
        t0 = xb
        st0 = sb("st0", [P, T, 6])
        mv0 = sb("mv0", [P, T, 2])
        ve0 = sb("ve0", [P, T])
        rstd0 = sb("rstd0", [P, T])
        y = sb("y", [P, T, P])
        ty = sb("ty", [P, T, P])
        yTh = sb("yTh", [P, B, N], fp16)
        yTl = sb("yTl", [P, B, N], fp16)
        aw = sb("aw", [P, 3 * P + E])
        awh = sb("awh", [P, 3 * P + E], fp16)
        awl = sb("awl", [P, 3 * P + E], fp16)
        kT = sb("kT", [P, B, N])
        qT = sb("qT", [P, B, N])
        val = sb("val", [P, T, P])
        vals = val
        LW = N + (A - 1) * P
        nmax1 = sb("nmax1", [P, T])
        sum1 = sb("sum1", [P, T])
        rec1 = sb("rec1", [P, T])
        prob1 = sb("prob1", [P, B, LW])
        t1 = sb("t1", [P, T, P])
        st1 = sb("st1", [P, T, 6])
        mv1 = sb("mv1", [P, T, 2])
        ve1 = sb("ve1", [P, T])
        rstd1 = sb("rstd1", [P, T])
        z = sb("z", [P, T, P])
        acc = sb("acc", [P, B, N])
        zh = sb("zh", [P, B, N], fp16)
        zl = sb("zl", [P, B, N], fp16)
        rl = sb("rl", [P, T, E])
        top = sb("top", [P, T, TOPS])
        topi = sb("topi", [P, T, TOPS], u32)
        topf = sb("topf", [P, T, 2])
        gap = sb("gap", [P, T, 1])
        tanh = sb("tanh", [P, T, 1])
        g1 = sb("g1", [P, T, 1])
        g2 = sb("g2", [P, T, 1])
        oh1 = sb("oh1", [P, T, E])
        oh2 = sb("oh2", [P, T, E])
        gw1 = sb("gw1", [P, T, E])
        gw2 = sb("gw2", [P, T, E])
        gate = sb("gate", [P, T, E])
        gateT = sb("gateT", [E, NH, HN])
        gates = sb("gates", [P, E, HN])
        W1f = sb("W1f", [P, E, F])
        W2f = sb("W2f", [P, E, F])
        W1h = sb("W1h", [P, E, F], fp16)
        W1l = sb("W1l", [P, E, F], fp16)
        W2h = sb("W2h", [P, E, F], fp16)
        W2l = sb("W2l", [P, E, F], fp16)
        hid = sb("hid", [P, HB, HN])
        hidh = sb("hidh", [P, HB, HN], fp16)
        hidl = sb("hidl", [P, HB, HN], fp16)
        gated = sb("gated", [P, 2, HN])
        gate_tiles = [gates, W1f]

        bank = [ctx.enter_context(nc.psum_tensor(f"bank{i}", [P, 512], fp32)) for i in range(8)]
        pS = pPT = pU = pYT = pKQ = pL = pR = pZ = bank[0:4]
        pV = [bank[4], bank[5], bank[4], bank[5]]
        pFG = bank[0:4]
        pX = [bank[5], bank[4]]
        pHV = [bank[6], bank[6]]
        pRT = [bank[6], bank[2]]
        pCT = [bank[7], bank[3]]
        pWF, pBN, pWV, pFOLD = bank[2], bank[3], bank[4], bank[6]
        pWARM = bank[7]
        pUP = [bank[0], bank[1]]
        pDN = [bank[6], bank[7]]

        x_in = [sem(f"x_in{h}") for h in range(NH)]
        wfg_in = sem("wfg_in")
        bn_in = sem("bn_in")
        bn_g_in = sem("bn_g_in")
        bias_in = sem("bias_in")
        wvh_in = sem("wvh_in")
        bias_row_in = sem("bias_row_in")
        attnw_in = sem("attnw_in")
        w_in = [sem(f"w_in{e}") for e in range(E)]
        zero_set = sem("zero_set")
        warm_set = sem("warm_set")
        ident_set = sem("ident_set")
        mask_set = sem("mask_set")
        ones_set = sem("ones_set")
        consts_set = sem("consts_set")
        iota_set = sem("iota_set")
        wfT_done = sem("wfT_done")
        wfT_ready = sem("wfT_ready")
        bnT_done = sem("bnT_done")
        bn_cols_ready = sem("bn_cols_ready")
        wvT_done = sem("wvT_done")
        wvT_ready = sem("wvT_ready")
        bh_widened = sem("bh_widened")
        fold_done = sem("fold_done")
        fold_ready = sem("fold_ready")
        bn_var_ready = sem("bn_var_ready")
        bn_inv_ready = sem("bn_inv_ready")
        bn_step = sem("bn_step")
        bn_ready = sem("bn_ready")
        xT_done = sem("xT_done")
        xb_ready = sem("xb_ready")
        fg_done = sem("fg_done")
        fg_ready = sem("fg_ready")
        fgh_ready = sem("fgh_ready")
        fg3_ready = sem("fg3_ready")
        xh_ready = sem("xh_ready")
        xl_ready = sem("xl_ready")
        foldh_ready = sem("foldh_ready")
        foldl_ready = sem("foldl_ready")
        wfg_step = sem("wfg_step")
        awh_ready = sem("awh_ready")
        awl_ready = sem("awl_ready")
        hv_done = sem("hv_done")
        hv_ready = sem("hv_ready")
        s_done = sem("s_done")
        nmax0_ready = sem("nmax0_ready")
        prob0_ready = sem("prob0_ready")
        rec0_ready = sem("rec0_ready")
        pT_done = sem("pT_done")
        prob0T_ready = sem("prob0T_ready")
        u_done = sem("u_done")
        t0_ready = sem("t0_ready")
        st0_ready = sem("st0_ready")
        mv0_ready = sem("mv0_ready")
        ve0_ready = sem("ve0_ready")
        rstd0_ready = sem("rstd0_ready")
        y_ready = sem("y_ready")
        ty_ready = sem("ty_ready")
        yT_done = sem("yT_done")
        yTh_ready = sem("yTh_ready")
        yTl_ready = sem("yTl_ready")
        kq_done = sem("kq_done")
        kq_ready = sem("kq_ready")
        v_done = sem("v_done")
        val_ready = sem("val_ready")
        l_done = sem("l_done")
        nmax1_ready = sem("nmax1_ready")
        prob1_ready = sem("prob1_ready")
        rec1_ready = sem("rec1_ready")
        vals_ready = sem("vals_ready")
        r_done = sem("r_done")
        t1_ready = sem("t1_ready")
        st1_ready = sem("st1_ready")
        mv1_ready = sem("mv1_ready")
        ve1_ready = sem("ve1_ready")
        rstd1_ready = sem("rstd1_ready")
        z_ready = sem("z_ready")
        zT_done = sem("zT_done")
        acc_ready = sem("acc_ready")
        zh_ready = sem("zh_ready")
        zl_ready = sem("zl_ready")
        rt_done = sem("rt_done")
        rl_ready = sem("rl_ready")
        top_ready = sem("top_ready")
        topi_ready = sem("topi_ready")
        topf_ready = sem("topf_ready")
        gap_ready = sem("gap_ready")
        tanh_ready = sem("tanh_ready")
        g_ready = sem("g_ready")
        oh_ready = sem("oh_ready")
        gw_ready = sem("gw_ready")
        gate_ready = sem("gate_ready")
        gateT_done = sem("gateT_done")
        gateT_ready = sem("gateT_ready")
        gates_out = [sem(f"gates_out{h}") for h in range(NH)]
        gates_in = [sem(f"gates_in{d}") for d in range(SUMS)]
        wh_ready = sem("wh_ready")
        wl_ready = sem("wl_ready")
        up_done = sem("up_done")
        hid_ready = sem("hid_ready")
        high_act = sem("high_act")
        high_dve = sem("high_dve")
        low_pool = sem("low_pool")
        low_dve = sem("low_dve")
        down_done = sem("down_done")
        gated_ready = sem("gated_ready")
        acc_added = sem("acc_added")
        out_stored = sem("out_stored")

        block = ctx.enter_context(nc.Block())

        def made(sems, chunks, h, e, c):
            mine = c in chunks[h]
            per = [len(q) if mine else FC - len(q) for q in chunks]
            return sems[0 if mine else 1], (h * E * per[0] + e * per[h]
                                            + sum((q in chunks[h]) == mine for q in range(c + 1)))

        def high_part(h, e, c):
            return made((high_act, high_dve), ACT_HIGH, h, e, c)

        def low_part(h, e, c):
            return made((low_pool, low_dve), POOL_LOW, h, e, c)

        def unit_before(h, e, c, back):
            c -= back
            while c < 0:
                c += FC
                if isinstance(e, int) and e == 0:
                    if h == 0:
                        return None
                    h, e = h - 1, E - 1
                else:
                    e = e - 1
            return h, e, c

        def experts_of_second_half(eng, unit):
            for e in range(2):
                for c in range(FC):
                    unit(1, e, c, e)
            with eng.Fori(2, E - 1, 2) as e:
                for j in range(2):
                    for c in range(FC):
                        unit(1, e + j, c, j)

        BN_IN = 16 * 6
        BN_G_IN = 16 * 4
        BIAS_IN = 16 * 3
        ATTNW_IN = 16 * 4

        @block.sync
        def _(sync):
            sync.dma_start(xT[:, half(0), :], x_v[:, half(0), :]).then_inc(x_in[0], 16)
            sync.dma_start(wf_s[:, :], wf).then_inc(wfg_in, 16)
            for k, v in enumerate((bf, gf, betaf, mf, vf, bg)):
                sync.dma_start(bn_rows4[k:k + 1, :, :], per_batch(v)).then_inc(bn_in, 16)
            sync.dma_start(xT[:, half(1), :], x_v[:, half(1), :]).then_inc(x_in[1], 16)
            sync.dma_start(wv_s[:, :], wv).then_inc(wvh_in, 16)
            sync.dma_start(wh_s[:, :], wh).then_inc(wvh_in, 16)
            sync.dma_start(bias_rows4[2:3, :, :], per_batch(bh)).then_inc(bias_in, 16)
            sync.dma_start(bv_row[:, :], row(bv)).then_inc(bias_row_in, 16)
            sync.dma_start(bvalue_row[:, :], row(bvalue)).then_inc(bias_row_in, 16)
            sync.dma_start(bias_rows[0:1, :], row(bk)).then_inc(bias_in, 16)
            sync.dma_start(bias_rows[1:2, :], row(bq)).then_inc(bias_in, 16)
            for k, w in enumerate((Wk, Wq, Wv, Wgate)):
                sync.dma_start(aw[:, k * P:k * P + w.shape[1]], w).then_inc(attnw_in, 16)
            for e in range(E):
                sync.dma_start(W1f[:, e, :], W1[e, :, :]).then_inc(w_in[e], 16)
                sync.dma_start(W2f[:, e, :].rearrange("p (c d) -> p c d", c=FC),
                               W2[e, :, :].rearrange("(c p) d -> p c d", p=P)).then_inc(w_in[e], 16)
            for h in range(NH):
                sync.wait_ge(gateT_ready, h + 1)
                sync.dma_start(gates_dram[h, :, :], gateT[:, h, :]).then_inc(gates_out[h], 16)
                sync.wait_ge(gates_out[h], 16)
                if h == 1:
                    sync.wait_ge(wl_ready, 2 * E)
                for e in range(E):
                    sync.dma_start(gate_tiles[h][:, e, :],
                                   gates_dram[h, e:e + 1, :].broadcast_to([P, HN])).then_inc(gates_in[h * E + e], 16)
            for h in range(NH):
                sync.wait_ge(acc_added, (h + 1) * E)
                sync.dma_start(out_v[:, half(h), :], acc[:, half(h), :]).then_inc(out_stored, 16)
            sync.wait_ge(out_stored, 16 * NH)

        @block.gpsimd
        def _(pool):
            pool.memset(warm_b[:, :], 0.0).then_inc(warm_set, 1)
            pool.memset(ident[:, :], 0.0).then_inc(zero_set, 1)
            pool.wait_ge(zero_set, 1)
            pool.affine_select(out=ident[:, :], in_=ident[:, :], compare_op=ALU.not_equal, fill=1.0,
                               base=0, pattern=[[-1, P]], channel_multiplier=1).then_inc(ident_set, 1)
            for k, v in enumerate((gg, betag, mg, vg)):
                pool.dma_start(bn_rows4[6 + k:7 + k, :, :], per_batch(v)).then_inc(bn_g_in, 16)
            pool.memset(power[:, :], -0.5).then_inc(consts_set, 1)
            pool.memset(qscale[:, 0:1], float(MID) ** -0.5).then_inc(consts_set, 1)
            pool.memset(qscale[:, 1:2], 1.0).then_inc(consts_set, 1)
            pool.memset(ones[:, :], 1.0).then_inc(ones_set, 1)
            pool.memset(identb[:, :], 0.0).then_inc(zero_set, 1)
            pool.memset(maskb[:, :], 0.0).then_inc(zero_set, 1)
            pool.wait_ge(zero_set, 3)
            pool.affine_select(out=identb[:, :], in_=identb[:, :], compare_op=ALU.not_equal, fill=1.0,
                               base=0, pattern=[[-1, P]], channel_multiplier=1).then_inc(ident_set, 1)
            pool.affine_select(out=maskb[:, :], in_=maskb[:, :], compare_op=ALU.is_ge, fill=NEG,
                               base=0, pattern=[[1, P]], channel_multiplier=-1).then_inc(mask_set, 1)
            pool.iota(iota_e[:, :], pattern=[[1, E]], base=0, channel_multiplier=0,
                      allow_small_or_imprecise_dtypes=True).then_inc(iota_set, 1)

            def bn_pow(_):
                par = bn_cols[:, :].rearrange("p (w k) -> p w k", k=5)
                pool.wait_ge(bn_cols_ready, 1)
                pool.wait_ge(consts_set, 3)
                pool.tensor_scalar(bn_var[:, :], par[:, :, 4], BN_EPS, None, ALU.add).then_inc(bn_var_ready, 1)
                pool.wait_ge(bn_var_ready, 1)
                pool.tensor_tensor(bn_inv[:, :], bn_var[:, :], power[:, :], ALU.pow).then_inc(bn_inv_ready, 1)

            def rstd(b, mv, ve, rs, mv_ready, ve_ready, rs_ready):
                r = slice(A * b, A * b + A)
                pool.wait_ge(mv_ready, b + 1)
                pool.tensor_scalar(ve[:, r], mv[:, r, 1], LN_EPS, None, ALU.add).then_inc(ve_ready, 1)
                pool.wait_ge(ve_ready, b + 1)
                pool.tensor_tensor(rs[:, r], ve[:, r], power[:, 0:A], ALU.pow).then_inc(rs_ready, 1)

            def rstd_0(b):
                rstd(b, mv0, ve0, rstd0, mv0_ready, ve0_ready, rstd0_ready)

            def residual(b):
                r = slice(A * b, A * b + A)
                pool.wait_ge(y_ready, b + 1)
                pool.tensor_tensor(ty[:, r, :], t0[:, r, :], y[:, r, :], ALU.add).then_inc(ty_ready, 1)

            def rstd_1(b):
                rstd(b, mv1, ve1, rstd1, mv1_ready, ve1_ready, rstd1_ready)

            def unit(h, e, c, parity):
                if c not in POOL_LOW[h]:
                    return
                n = (h * E + e) * FC + c
                pool.wait_ge(*high_part(h, e, c))
                if unit_before(h, e, c, HB):
                    pool.wait_ge(down_done, n - HB + 1)
                pool.tensor_tensor(hidl[:, c, :], hid[:, c, :], hidh[:, c, :],
                                   ALU.subtract).then_inc(low_pool, 1)

            def branches_low(b):
                pool.wait_ge(fgh_ready, b + 1)
                for w, r in ((0, 2), (1, 1)):
                    q = slice(r * MID, (r + 1) * MID)
                    last = pool.tensor_tensor(fg3[q, b, w, :], fg[q, b % 2, w, :], fg3[q, b, w, :], ALU.subtract)
                last.then_inc(fg3_ready, 1)

            steps = {"branches_low": branches_low, "bn_pow": bn_pow, "rstd0": rstd_0, "residual": residual, "rstd1": rstd_1,
                     "unit": lambda n: unit(0, n // FC, n % FC, n // FC % 2)}
            for step, k in order(steps, 4.6):
                steps[step](k)
            experts_of_second_half(pool, unit)

        @block.scalar
        def _(act):
            act.dma_start(wg_s[:, :], wg).then_inc(wfg_in, 16)

            def tokens_high(h):
                act.wait_ge(x_in[h], 16)
                act.activation(xh[:, half(h), :], xT[:, half(h), :], ACT.Copy).then_inc(xh_ready, 1)

            def attention_high(_):
                act.wait_ge(attnw_in, ATTNW_IN)
                act.activation(awh[:, :], aw[:, :], ACT.Copy, scale=WS).then_inc(awh_ready, 1)

            def branch_copy(h):
                r = slice(h * HT, (h + 1) * HT)
                act.wait_ge(hv_done, h + 1)
                act.activation(hv[:, r, :].rearrange("p t n -> p (t n)"), pHV[h][:, :], ACT.Copy,
                               scale=1.0 / WS).then_inc(hv_ready, 1)

            def relus(b):
                act.wait_ge(fg_done, b + 1)
                act.wait_ge(bn_ready, 1)
                if b >= 2:
                    act.wait_ge(fg3_ready, b - 1)
                for w in range(2):
                    last = act.activation(fg[:, b % 2, w, :], pFG[b][0:MK, w * N:(w + 1) * N], ACT.Relu,
                                          bias=bn_bias[0:MK, w:w + 1], scale=bn_scale_w[0:MK, w:w + 1])
                last.then_inc(fg_ready, 1)

            def exp_0(b):
                act.wait_ge(nmax0_ready, b + 1)
                for a in range(A):
                    i = A * b + a
                    act.activation(prob0[:, i, :], pS[b][:, a * N:(a + 1) * N], ACT.Exp,
                                   bias=nmax0[:, i:i + 1], accum_out=sum0[:, i:i + 1]).then_inc(prob0_ready, 1)

            def probsT_copy(b):
                act.wait_ge(pT_done, b + 1)
                act.activation(prob0T[:, A * b:A * b + A, :].rearrange("p a n -> p (a n)"),
                               pPT[b][:, :], ACT.Copy).then_inc(prob0T_ready, 1)

            def norm_high(b):
                act.wait_ge(yT_done, b + 1)
                act.activation(yTh[:, b, :], pYT[b][:, 0:N], ACT.Copy, scale=XS).then_inc(yTh_ready, 1)

            def keys_copy(b):
                act.wait_ge(kq_done, b + 1)
                act.activation(kT[:, b, :], pKQ[b][:, 0:N], ACT.Identity,
                               scale=1.0 / (XS * WS), bias=bias_cols[:, 0:1]).then_inc(kq_ready, 1)
                act.activation(qT[:, b, :], pKQ[b][:, N:2 * N], ACT.Identity,
                               scale=1.0 / (XS * WS), bias=bias_cols[:, 1:2]).then_inc(kq_ready, 1)

            def exp_1(b):
                act.wait_ge(nmax1_ready, A * (b + 1))
                for a in range(A):
                    i = A * b + a
                    lo, hi = (0, N) if a == 0 else (N, LW)
                    act.activation(prob1[:, b, lo:hi], pL[b][:, lo:hi], ACT.Exp,
                                   bias=nmax1[:, i:i + 1], accum_out=sum1[:, i:i + 1]).then_inc(prob1_ready, 1)

            def final_copy(b):
                act.wait_ge(zT_done, b + 1)
                act.activation(zh[:, b, :], pZ[b][:, 0:N], ACT.Copy, scale=XS).then_inc(zh_ready, 1)
                act.activation(acc[:, b, :], pZ[b][:, N:2 * N], ACT.Copy).then_inc(acc_ready, 1)

            def tanhs(h):
                act.wait_ge(gap_ready, h + 1)
                act.activation(tanh[:, h * HT:(h + 1) * HT, :], gap[:, h * HT:(h + 1) * HT, :],
                               ACT.Tanh, scale=0.5 / (XS * WS)).then_inc(tanh_ready, 1)

            def gatesT_copy(h):
                act.wait_ge(gateT_done, h + 1)
                act.activation(gateT[:, h, :], pCT[h][0:E, :], ACT.Copy).then_inc(gateT_ready, 1)

            def weights(e):
                act.wait_ge(w_in[e], 32)
                act.activation(W1h[:, e, :], W1f[:, e, :], ACT.Copy, scale=WS).then_inc(wh_ready, 1)
                act.activation(W2h[:, e, :], W2f[:, e, :], ACT.Copy, scale=WS).then_inc(wh_ready, 1)

            def unit(h, e, c, parity):
                n = (h * E + e) * FC + c
                act.wait_ge(up_done, n + 1)
                if unit_before(h, e, c, HB):
                    act.wait_ge(*low_part(*unit_before(h, e, c, HB)))
                act.activation(hid[:, c, :], pUP[c % 2][:, :], ACT.Silu,
                               scale=1.0 / (XS * WS)).then_inc(hid_ready, 1)
                if c in ACT_HIGH[h]:
                    act.wait_ge(hid_ready, n + 1)
                    if unit_before(h, e, c, HB):
                        act.wait_ge(down_done, n - HB + 1)
                    act.activation(hidh[:, c, :], hid[:, c, :], ACT.Copy).then_inc(high_act, 1)

            steps = {"tokens_high": tokens_high, "branch_copy": branch_copy, "attention_high": attention_high, "norm_high": norm_high,
                     "relus": relus, "exp0": exp_0, "probsT_copy": probsT_copy, "keys_copy": keys_copy,
                     "exp1": exp_1, "final_copy": final_copy, "tanh": tanhs, "gatesT_copy": gatesT_copy,
                     "weights": weights,
                     "unit": lambda n: unit(0, n // FC, n % FC, n // FC % 2)}
            for step, k in order(steps, 3.2):
                steps[step](k)
            experts_of_second_half(act, unit)

        @block.vector
        def _(dve):
            def convs_copy(_):
                dve.wait_ge(wfT_done, 1)
                src = pWF[:, 0:2 * MID].rearrange("p (w m) -> p w m", w=2)
                for r in range(3):
                    last = dve.tensor_scalar(wfgT[:, :, r, :], src, WS, None, ALU.mult)
                last.then_inc(wfg_step, 1)
                dve.wait_ge(wfg_step, 1)
                flat = wfgT[:, :, :, :].rearrange("p w r m -> p (w r m)")
                flath = wfgTh[:, :, :].rearrange("p w m -> p (w m)")
                flatl = wfgTl[:, :, :].rearrange("p w m -> p (w m)")
                dve.tensor_copy(flath, flat).then_inc(wfg_step, 1)
                dve.wait_ge(wfg_step, 2)
                dve.tensor_tensor(flatl, flat, flath, ALU.subtract).then_inc(wfT_ready, 1)

            def bn_copy(_):
                dve.wait_ge(bnT_done, 1)
                dve.tensor_copy(bn_cols[:, :], pBN[:, 0:10]).then_inc(bn_cols_ready, 1)
                dve.wait_ge(consts_set, 3)
                dve.wait_ge(bn_cols_ready, 1)
                par = bn_cols[:, :].rearrange("p (w k) -> p w k", k=5)
                dve.tensor_tensor(bn_gain[:, :], par[:, :, 1], qscale[:, :], ALU.mult).then_inc(bn_step, 1)
                dve.tensor_tensor(bn_off[:, :], par[:, :, 0], par[:, :, 3], ALU.subtract).then_inc(bn_step, 1)
                dve.tensor_tensor(bn_beta[:, :], par[:, :, 2], qscale[:, :], ALU.mult).then_inc(bn_step, 1)

            def bn_fold(_):
                dve.wait_ge(bn_inv_ready, 1)
                dve.wait_ge(bn_step, 3)
                dve.tensor_tensor(bn_scale[:, :], bn_inv[:, :], bn_gain[:, :], ALU.mult).then_inc(bn_step, 1)
                dve.wait_ge(bn_step, 4)
                dve.tensor_tensor(bn_move[:, :], bn_off[:, :], bn_scale[:, :], ALU.mult).then_inc(bn_step, 1)
                dve.wait_ge(bn_step, 5)
                dve.tensor_scalar(bn_scale_w[:, :], bn_scale[:, :], 1.0 / WS, None, ALU.mult).then_inc(bn_step, 1)
                dve.wait_ge(bn_step, 6)
                dve.tensor_tensor(bn_bias[:, :], bn_move[:, :], bn_beta[:, :], ALU.add).then_inc(bn_ready, 1)

            def tokens_split(h):
                dve.wait_ge(xh_ready, h + 1)
                dve.tensor_tensor(xl[:, half(h), :], xT[:, half(h), :], xh[:, half(h), :],
                                  ALU.subtract).then_inc(xl_ready, 1)

            def attention_low(_):
                dve.wait_ge(awh_ready, 1)
                dve.scalar_tensor_tensor(out=awl[:, :], in0=aw[:, :], scalar=WS, in1=awh[:, :],
                                         op0=ALU.mult, op1=ALU.subtract).then_inc(awl_ready, 1)

            def branches_high(b):
                dve.wait_ge(fg_ready, b + 1)
                dve.tensor_copy(fg3[:, b, :, :].rearrange("p w n -> p (w n)"),
                                fg[:, b % 2, :, :].rearrange("p w n -> p (w n)")).then_inc(fgh_ready, 1)

            def fold_prepare(_):
                dve.wait_ge(wvT_done, 1)
                dve.tensor_copy(bias_cols[:, :], pWV[:, P:P + 3]).then_inc(wvT_ready, 1)
                dve.tensor_copy(wvT[:, :], pWV[0:MID, 0:P]).then_inc(wvT_ready, 1)
                dve.wait_ge(wvT_ready, 1)
                dve.wait_ge(ones_set, 1)
                dve.tensor_scalar(bh_wide[:, :], ones[0:MID, :], bias_cols[0:MID, 2:3], None,
                                  ALU.mult).then_inc(bh_widened, 1)

            def fold_copy(_):
                dve.wait_ge(fold_done, 1)
                dve.tensor_scalar(foldh[:, :], pFOLD[:, 0:P], WS, None, ALU.mult).then_inc(foldh_ready, 1)
                dve.tensor_copy(fold[:, :, :].rearrange("p k n -> p (k n)"), pFOLD[:, 0:3 * P]).then_inc(fold_ready, 1)
                dve.wait_ge(foldh_ready, 1)
                dve.wait_ge(fold_ready, 1)
                dve.scalar_tensor_tensor(out=foldl[:, :], in0=fold[:, 0, :], scalar=WS, in1=foldh[:, :],
                                         op0=ALU.mult, op1=ALU.subtract).then_inc(foldl_ready, 1)

            def tokens_copy(h):
                r = slice(h * HT, (h + 1) * HT)
                dve.wait_ge(xT_done, h + 1)
                dve.wait_ge(fold_ready, 1)
                dve.tensor_tensor(xb[:, r, :], pX[h][:, :].rearrange("p (t n) -> p t n", n=P),
                                  fold[:, 1:2, :].broadcast_to([P, HT, P]), ALU.add).then_inc(xb_ready, 1)

            def max_0(b):
                dve.wait_ge(s_done, b + 1)
                dve.tensor_reduce(nmax0[:, A * b:A * b + A], pS[b][:, :].rearrange("p (a n) -> p a n", a=A),
                                  AX.X, ALU.max, negate=True).then_inc(nmax0_ready, 1)

            def stats(b, src, st, src_ready, count, st_ready):
                dve.wait_ge(src_ready, count)
                for i in range(A * b, A * b + A):
                    last = dve.bn_stats(st[:, i, :], src[:, i, :])
                last.then_inc(st_ready, 1)

            def aggregate(b, st, mv, st_ready, mv_ready):
                dve.wait_ge(st_ready, b + 1)
                for i in range(A * b, A * b + A):
                    last = dve.bn_aggr(mv[:, i, :], st[:, i, :])
                last.then_inc(mv_ready, 1)

            def normalize(b, src, mv, rs, dst, mv_ready, rs_ready, dst_ready):
                dve.wait_ge(mv_ready, b + 1)
                dve.wait_ge(rs_ready, b + 1)
                for i in range(A * b, A * b + A):
                    last = dve.tensor_scalar(dst[:, i, :], src[:, i, :], mv[:, i, 0:1], rs[:, i:i + 1],
                                             ALU.subtract, ALU.mult)
                last.then_inc(dst_ready, 1)

            def rec_0(b):
                dve.wait_ge(prob0_ready, A * (b + 1))
                dve.reciprocal(rec0[:, A * b:A * b + A], sum0[:, A * b:A * b + A]).then_inc(rec0_ready, 1)

            def add_0(b):
                dve.wait_ge(u_done, b + 1)
                dve.wait_ge(rec0_ready, b + 1)
                dve.wait_ge(xb_ready, b // HBT + 1)
                for a in range(A):
                    i = A * b + a
                    dve.scalar_tensor_tensor(out=t0[:, i, :], in0=pU[b][:, a * P:(a + 1) * P],
                                             scalar=rec0[:, i:i + 1], in1=xb[:, i, :],
                                             op0=ALU.mult, op1=ALU.add).then_inc(t0_ready, 1)

            def stats_0(b):
                stats(b, t0, st0, t0_ready, A * (b + 1), st0_ready)

            def aggr_0(b):
                aggregate(b, st0, mv0, st0_ready, mv0_ready)

            def norm_0(b):
                normalize(b, t0, mv0, rstd0, y, mv0_ready, rstd0_ready, y_ready)

            def normT_copy(b):
                dve.wait_ge(yTh_ready, b + 1)
                dve.scalar_tensor_tensor(out=yTl[:, b, :], in0=pYT[b][:, 0:N], scalar=XS, in1=yTh[:, b, :],
                                         op0=ALU.mult, op1=ALU.subtract).then_inc(yTl_ready, 1)

            def values_copy(b):
                dve.wait_ge(v_done, b + 1)
                dve.scalar_tensor_tensor(out=val[:, A * b:A * b + A, :],
                                         in0=pV[b][:, 0:A * P].rearrange("p (a n) -> p a n", a=A),
                                         scalar=1.0 / (XS * WS), in1=fold[:, 2:3, :].broadcast_to([P, A, P]),
                                         op0=ALU.mult, op1=ALU.add).then_inc(val_ready, 1)

            def max_1(b):
                dve.wait_ge(l_done, b + 1)
                for a in range(A):
                    i = A * b + a
                    lo, hi = (0, N) if a == 0 else (N, LW)
                    dve.tensor_reduce(nmax1[:, i:i + 1], pL[b][:, lo:hi], AX.X, ALU.max,
                                      negate=True).then_inc(nmax1_ready, 1)

            def rec_1(b):
                dve.wait_ge(prob1_ready, A * (b + 1))
                dve.reciprocal(rec1[:, A * b:A * b + A], sum1[:, A * b:A * b + A]).then_inc(rec1_ready, 1)

            def scale_values(b):
                dve.wait_ge(rec1_ready, b + 1)
                dve.wait_ge(val_ready, b + 1)
                for i in range(A * b, A * b + A):
                    last = dve.tensor_scalar(vals[:, i, :], val[:, i, :], rec1[:, i:i + 1],
                                             float(P) ** -0.5, ALU.mult, ALU.mult)
                last.then_inc(vals_ready, 1)

            def add_1(b):
                dve.wait_ge(r_done, b + 1)
                dve.wait_ge(ty_ready, b + 1)
                dve.tensor_tensor(t1[:, A * b:A * b + A, :].rearrange("p a n -> p (a n)"),
                                  pR[b][:, 0:A * P],
                                  ty[:, A * b:A * b + A, :].rearrange("p a n -> p (a n)"),
                                  ALU.add).then_inc(t1_ready, 1)

            def stats_1(b):
                stats(b, t1, st1, t1_ready, b + 1, st1_ready)

            def aggr_1(b):
                aggregate(b, st1, mv1, st1_ready, mv1_ready)

            def norm_1(b):
                normalize(b, t1, mv1, rstd1, z, mv1_ready, rstd1_ready, z_ready)

            def tokens_low(b):
                dve.wait_ge(zh_ready, b + 1)
                dve.wait_ge(acc_ready, b + 1)
                dve.scalar_tensor_tensor(out=zl[:, b, :], in0=pZ[b][:, 0:N], scalar=XS, in1=zh[:, b, :],
                                         op0=ALU.mult, op1=ALU.subtract).then_inc(zl_ready, 1)

            def route_copy(h):
                r = slice(h * HT, (h + 1) * HT)
                dve.wait_ge(rt_done, h + 1)
                dve.tensor_copy(rl[:, r, :].rearrange("p t e -> p (t e)"), pRT[h][:, 0:HT * E]).then_inc(rl_ready, 1)

            def top_two(h):
                r = slice(h * HT, (h + 1) * HT)
                dve.wait_ge(rl_ready, h + 1)
                for i in range(h * HT, (h + 1) * HT):
                    dve.max(top[:, i, :], rl[:, i, :]).then_inc(top_ready, 1)
                dve.wait_ge(top_ready, (h + 1) * HT)
                dve.tensor_tensor(gap[:, r, :], top[:, r, 1:2], top[:, r, 0:1], ALU.subtract).then_inc(gap_ready, 1)
                for i in range(h * HT, (h + 1) * HT):
                    dve.max_index(topi[:, i, :], top[:, i, :], rl[:, i, :]).then_inc(topi_ready, 1)

            def one_hots(h):
                r = slice(h * HT, (h + 1) * HT)
                dve.wait_ge(topi_ready, (h + 1) * HT)
                dve.tensor_copy(topf[:, r, :], topi[:, r, 0:2]).then_inc(topf_ready, 1)
                dve.wait_ge(topf_ready, h + 1)
                dve.wait_ge(iota_set, 1)
                lane = iota_e[:, :].unsqueeze(1).broadcast_to([P, HT, E])
                dve.tensor_tensor(oh1[:, r, :], topf[:, r, 0:1].broadcast_to([P, HT, E]), lane,
                                  ALU.is_equal).then_inc(oh_ready, 1)
                dve.tensor_tensor(oh2[:, r, :], topf[:, r, 1:2].broadcast_to([P, HT, E]), lane,
                                  ALU.is_equal).then_inc(oh_ready, 1)

            def gate_tokens(h):
                r = slice(h * HT, (h + 1) * HT)
                dve.wait_ge(tanh_ready, h + 1)
                dve.tensor_scalar(g1[:, r, :], tanh[:, r, :], -0.5 / WS, 0.5 / WS, ALU.mult, ALU.add).then_inc(g_ready, 1)
                dve.tensor_scalar(g2[:, r, :], tanh[:, r, :], 0.5 / WS, 0.5 / WS, ALU.mult, ALU.add).then_inc(g_ready, 1)
                dve.wait_ge(g_ready, 2 * (h + 1))
                dve.wait_ge(oh_ready, 2 * (h + 1))
                dve.tensor_tensor(gw1[:, r, :], oh1[:, r, :], g1[:, r, :].broadcast_to([P, HT, E]),
                                  ALU.mult).then_inc(gw_ready, 1)
                dve.tensor_tensor(gw2[:, r, :], oh2[:, r, :], g2[:, r, :].broadcast_to([P, HT, E]),
                                  ALU.mult).then_inc(gw_ready, 1)
                dve.wait_ge(gw_ready, 2 * (h + 1))
                dve.tensor_tensor(gate[:, r, :], gw1[:, r, :], gw2[:, r, :], ALU.add).then_inc(gate_ready, 1)

            def weights_low(e):
                for k, (wl, w, whi) in enumerate(((W1l, W1f, W1h), (W2l, W2f, W2h))):
                    dve.wait_ge(wh_ready, 2 * e + k + 1)
                    dve.scalar_tensor_tensor(out=wl[:, e, :], in0=w[:, e, :], scalar=WS, in1=whi[:, e, :],
                                             op0=ALU.mult, op1=ALU.subtract).then_inc(wl_ready, 1)

            def gate_sum(h, e, parity):
                d = h * E + e
                a = acc[:, half(h), :].rearrange("p b n -> p (b n)")
                dve.wait_ge(down_done, (d + 1) * FC)
                dve.tensor_tensor(gated[:, parity, :], pDN[parity][:, :], gate_tiles[h][:, e, :],
                                  ALU.mult).then_inc(gated_ready, 1)
                dve.wait_ge(gated_ready, d + 1)
                dve.tensor_tensor(a, a, gated[:, parity, :], ALU.add).then_inc(acc_added, 1)

            def unit(h, e, c, parity):
                n = (h * E + e) * FC + c
                dve.wait_ge(hid_ready, n + 1)
                if unit_before(h, e, c, HB):
                    dve.wait_ge(down_done, n - HB + 1)
                if c not in ACT_HIGH[h]:
                    dve.tensor_copy(hidh[:, c, :], hid[:, c, :]).then_inc(high_dve, 1)
                if c not in POOL_LOW[h]:
                    dve.wait_ge(*high_part(h, e, c))
                    dve.tensor_tensor(hidl[:, c, :], hid[:, c, :], hidh[:, c, :],
                                      ALU.subtract).then_inc(low_dve, 1)
                done = unit_before(h, e, c, LAG + 1)
                if done and done[2] == FC - 1:
                    if isinstance(done[1], int):
                        dve.wait_ge(gates_in[done[0] * E + done[1]], 16)
                        if done[1] == 0:
                            dve.wait_ge(acc_ready, HBT * (done[0] + 1))
                    gate_sum(done[0], done[1], 1 - parity)

            steps = {"tokens_split": tokens_split, "attention_low": attention_low,
                     "branches_high": branches_high, "convs_copy": convs_copy, "bn_copy": bn_copy, "bn_fold": bn_fold,
                     "fold_prepare": fold_prepare, "fold_copy": fold_copy, "tokens_copy": tokens_copy,
                     "max0": max_0, "rec0": rec_0, "add0": add_0,
                     "stats0": stats_0, "aggr0": aggr_0, "norm0": norm_0, "normT_copy": normT_copy,
                     "values_copy": values_copy, "max1": max_1, "rec1": rec_1,
                     "scale_values": scale_values, "add1": add_1, "stats1": stats_1, "aggr1": aggr_1,
                     "norm1": norm_1, "tokens_low": tokens_low, "route_copy": route_copy,
                     "top_two": top_two, "one_hots": one_hots, "gate_tokens": gate_tokens,
                     "weights_low": weights_low,
                     "unit": lambda n: unit(0, n // FC, n % FC, n // FC % 2)}
            for step, k in order(steps, 1.9):
                steps[step](k)
            for e in range(1, E):
                dve.wait_ge(gates_in[E + e], 16)
            experts_of_second_half(dve, unit)
            gate_sum(1, E - 1, 1)

        @block.tensor
        def _(pe):
            def warm(count):
                for _ in range(count):
                    pe.matmul(pWARM[:, :], warm_b[:, 0:P], warm_b[:, :], start=True, stop=True)

            def warm_up(count):
                pe.wait_ge(warm_set, 1)
                warm(count)

            def convsT(_):
                pe.wait_ge(ident_set, 1)
                pe.wait_ge(wfg_in, 32)
                pe.transpose(pWF[:, 0:MID], wf_s[:, :], ident[0:MID, 0:MID])
                pe.transpose(pWF[:, MID:2 * MID], wg_s[:, :], ident[0:MID, 0:MID]).then_inc(wfT_done, 1)

            def split_product(o, ah, al, bh_, bl_):
                pe.matmul(o, ah, bh_, start=True, stop=False)
                pe.matmul(o, ah, bl_, start=False, stop=False)
                return pe.matmul(o, al, bh_, start=False, stop=True)

            def convs(b):
                pe.wait_ge(wfT_ready, 1)
                pe.wait_ge(bn_cols_ready, 1)
                pe.wait_ge(xl_ready, b // HBT + 1)
                pe.wait_ge(xh_ready, b // HBT + 1)
                for w in range(2):
                    last = split_product(pFG[b][0:MK, w * N:(w + 1) * N], wfgTh[:, w, :], wfgTl[:, w, :],
                                         xh[:, b, :], xl[:, b, :])
                last.then_inc(fg_done, 1)

            def bnT(_):
                pe.wait_ge(bn_in, BN_IN)
                pe.wait_ge(bn_g_in, BN_G_IN)
                pe.transpose(pBN[:, 0:10], bn_rows[:, :], ident[0:10, 0:10]).then_inc(bnT_done, 1)

            def foldT(_):
                pe.wait_ge(wvh_in, 32)
                pe.wait_ge(bias_in, BIAS_IN)
                pe.transpose(pWV[:, P:P + 3], bias_rows[:, :], ident[0:3, 0:3])
                pe.transpose(pWV[0:MID, 0:P], wv_s[:, :], ident[:, :]).then_inc(wvT_done, 1)

            def fold_convs(_):
                pe.wait_ge(wvT_ready, 2)
                pe.matmul(pFOLD[:, 0:P], wh_s[:, :], wvT[:, :], start=True, stop=True)
                pe.wait_ge(bh_widened, 1)
                pe.wait_ge(bias_row_in, 32)
                pe.matmul(pFOLD[:, P:2 * P], bh_wide[:, :], wvT[:, :], start=True, stop=False)
                pe.matmul(pFOLD[:, P:2 * P], ones[0:1, :], bv_row[:, :], start=False, stop=True)
                pe.matmul(pFOLD[:, 2 * P:3 * P], ones[0:1, :], bvalue_row[:, :], start=True,
                          stop=True).then_inc(fold_done, 1)

            def tokens(h):
                pe.wait_ge(x_in[h], 16)
                if h == 1:
                    pe.wait_ge(wvT_ready, 2)
                for i in range(HT):
                    b, a = h * HBT + i // A, i % A
                    last = pe.transpose(pX[h][:, i * P:(i + 1) * P], xT[:, b, a * P:(a + 1) * P], ident[:, :])
                last.then_inc(xT_done, 1)

            def branch(h):
                if h == 1:
                    pe.wait_ge(hv_ready, 1)
                pe.wait_ge(foldl_ready, 1)
                pe.wait_ge(xl_ready, h + 1)
                for i in range(HT):
                    b, t = h * HBT + i // A, slice(i % A * P, (i % A + 1) * P)
                    last = split_product(pHV[h][:, i * P:(i + 1) * P], xh[:, b, t], xl[:, b, t],
                                         foldh[:, :], foldl[:, :])
                last.then_inc(hv_done, 1)

            def scores(b):
                pe.wait_ge(fg3_ready, b + 1)
                for a in range(A):
                    last = pe.matmul(pS[b][:, a * N:(a + 1) * N], fg3[:, b, 0, a * P:(a + 1) * P],
                                     fg3[:, b, 1, :], start=True, stop=True)
                last.then_inc(s_done, 1)

            def probsT(b):
                pe.wait_ge(prob0_ready, A * (b + 1))
                for j in range(A):
                    for a in range(A):
                        col = j * N + a * P
                        last = pe.transpose(pPT[b][:, col:col + P],
                                            prob0[:, A * b + a, j * P:(j + 1) * P], ident[:, :])
                last.then_inc(pT_done, 1)

            def mix(b):
                pe.wait_ge(prob0T_ready, b + 1)
                pe.wait_ge(hv_ready, b // HBT + 1)
                for a in range(A):
                    for j in range(A):
                        last = pe.matmul(pU[b][:, a * P:(a + 1) * P],
                                         prob0T[:, A * b + j, a * P:(a + 1) * P], hv[:, A * b + j, :],
                                         start=(j == 0), stop=(j == A - 1))
                last.then_inc(u_done, 1)

            def normT(b):
                pe.wait_ge(y_ready, b + 1)
                for a in range(A):
                    last = pe.transpose(pYT[b][:, a * P:(a + 1) * P], y[:, A * b + a, :], ident[:, :])
                last.then_inc(yT_done, 1)

            def keys(b):
                pe.wait_ge(awl_ready, 1)
                pe.wait_ge(yTl_ready, b + 1)
                split_product(pKQ[b][:, 0:N], awh[:, 0:P], awl[:, 0:P], yTh[:, b, :], yTl[:, b, :])
                split_product(pKQ[b][:, N:2 * N], awh[:, P:2 * P], awl[:, P:2 * P],
                              yTh[:, b, :], yTl[:, b, :]).then_inc(kq_done, 1)

            def values(b):
                pe.wait_ge(*((val_ready, b - 1) if b >= 2 else (xb_ready, 2 - b)))
                for a in range(A):
                    t = slice(a * P, (a + 1) * P)
                    last = split_product(pV[b][:, t], yTh[:, b, t], yTl[:, b, t],
                                         awh[:, 2 * P:3 * P], awl[:, 2 * P:3 * P])
                last.then_inc(v_done, 1)

            def logits(b):
                pe.wait_ge(mask_set, 1)
                pe.wait_ge(ident_set, 2)
                pe.wait_ge(kq_ready, 2 * (b + 1))
                for a in range(A):
                    lo, hi = (0, N) if a == 0 else (N, LW)
                    pe.matmul(pL[b][:, lo:hi], kT[:, b, a * P:(a + 1) * P], qT[:, b, a * P:N],
                              start=True, stop=False)
                    last = pe.matmul(pL[b][:, lo:lo + P], identb[:, :], maskb[:, :],
                                     start=False, stop=True)
                last.then_inc(l_done, 1)

            def read(b):
                pe.wait_ge(prob1_ready, A * (b + 1))
                pe.wait_ge(vals_ready, b + 1)
                pe.matmul(pR[b][:, 0:P], prob1[:, b, 0:P], vals[:, A * b, :], start=True, stop=True)
                pe.matmul(pR[b][:, P:2 * P], prob1[:, b, P:N], vals[:, A * b, :], start=True, stop=False)
                pe.matmul(pR[b][:, P:2 * P], prob1[:, b, N:LW], vals[:, A * b + 1, :], start=False,
                          stop=True).then_inc(r_done, 1)

            def finalT(b):
                pe.wait_ge(z_ready, b + 1)
                for a in range(A):
                    i = A * b + a
                    pe.transpose(pZ[b][:, a * P:(a + 1) * P], z[:, i, :], ident[:, :])
                    last = pe.transpose(pZ[b][:, N + a * P:N + (a + 1) * P], t1[:, i, :], ident[:, :])
                last.then_inc(zT_done, 1)

            def route(h):
                pe.wait_ge(*((hv_ready, NH) if h == 0 else (zl_ready, B)))
                for i in range(HT):
                    b, a = h * HBT + i // A, i % A
                    pe.wait_ge(zl_ready, b + 1)
                    t = slice(a * P, (a + 1) * P)
                    last = split_product(pRT[h][:, i * E:(i + 1) * E], zh[:, b, t], zl[:, b, t],
                                         awh[:, 3 * P:3 * P + E], awl[:, 3 * P:3 * P + E])
                last.then_inc(rt_done, 1)

            def gatesT(h):
                pe.wait_ge(gate_ready, h + 1)
                for i in range(HT):
                    last = pe.transpose(pCT[h][0:E, i * P:(i + 1) * P], gate[:, h * HT + i, :], ident[:, :])
                last.then_inc(gateT_done, 1)

            def down(h, e, c, parity):
                pe.wait_ge(*low_part(h, e, c))
                if c == 0:
                    if isinstance(e, int) and h == 0 and e < 2:
                        pe.wait_ge(*((rl_ready, 1) if e == 0 else (gateT_ready, 1)))
                    else:
                        pe.wait_ge(gated_ready, h * E + e - 1)
                ch = slice(c * P, (c + 1) * P)
                o = pDN[parity][:, :]
                pe.matmul(o, W2h[:, e, ch], hidh[:, c, :], start=(c == 0), stop=False)
                pe.matmul(o, W2h[:, e, ch], hidl[:, c, :], start=False, stop=False)
                pe.matmul(o, W2l[:, e, ch], hidh[:, c, :], start=False,
                          stop=(c == FC - 1)).then_inc(down_done, 1)

            def unit(h, e, c, parity):
                if h == 0 and c == 0:
                    pe.wait_ge(wl_ready, 2 * e + 2)
                if isinstance(e, int) and e == 0 and c == 0:
                    pe.wait_ge(zl_ready, HBT * (h + 1))
                n = (h * E + e) * FC + c
                if unit_before(h, e, c, 2):
                    pe.wait_ge(hid_ready, n - 1)
                ch = slice(c * P, (c + 1) * P)
                th = zh[:, half(h), :].rearrange("p b n -> p (b n)")
                tl = zl[:, half(h), :].rearrange("p b n -> p (b n)")
                o = pUP[c % 2][:, :]
                pe.matmul(o, W1h[:, e, ch], th, start=True, stop=False)
                pe.matmul(o, W1h[:, e, ch], tl, start=False, stop=False)
                pe.matmul(o, W1l[:, e, ch], th, start=False, stop=True).then_inc(up_done, 1)
                m = unit_before(h, e, c, LAG)
                if m:
                    down(*m, parity if m[2] <= c else 1 - parity)

            steps = {"warm": warm, "convsT": convsT, "convs": convs, "bnT": bnT, "foldT": foldT, "fold": fold_convs,
                     "tokens": tokens, "branch": branch, "scores": scores, "probsT": probsT, "mix": mix,
                     "normT": normT, "keys": keys, "values": values, "logits": logits,
                     "read": read, "finalT": finalT, "route": route, "gatesT": gatesT,
                     "unit": lambda n: unit(0, n // FC, n % FC, n // FC % 2)}
            warm_up(WARM_UP)
            for step, k in order(steps, 0.0):
                steps[step](k)
            experts_of_second_half(pe, unit)
            for c in range(FC - LAG, FC):
                down(1, E - 1, c, (E - 1) % 2)


_INS = ['x', 'L0_conv_wf', 'L0_conv_bf', 'L0_conv_gf', 'L0_conv_betaf', 'L0_conv_mf', 'L0_conv_vf',
        'L0_conv_wg', 'L0_conv_bg', 'L0_conv_gg', 'L0_conv_betag', 'L0_conv_mg', 'L0_conv_vg',
        'L0_conv_wh', 'L0_conv_bh', 'L0_conv_wv', 'L0_conv_bv',
        'L1_attn_Wk', 'L1_attn_bk', 'L1_attn_Wq', 'L1_attn_bq', 'L1_attn_Wv', 'L1_attn_bv',
        'L1_ffn_Wg', 'L1_ffn_W1', 'L1_ffn_W2']
_OUTS = [((4, 128, 16, 16), 'float32')]


def kernel(**inputs):
    import numpy as _np
    import concourse.bacc as _bacc
    from concourse import mybir as _mybir
    from concourse.bass_utils import run_bass_kernel_spmd as _run

    nc = _bacc.Bacc("TRN2", target_bir_lowering=False, num_devices=1)
    arrays, args = {}, []
    for name in _INS:
        a = _np.ascontiguousarray(inputs[name])
        arrays[f"in_{name}_dram"] = a
        args.append(nc.dram_tensor(f"in_{name}_dram", a.shape, _mybir.dt.from_np(a.dtype), kind="ExternalInput").ap())
    for i, (shape, dtype) in enumerate(_OUTS):
        dt = _mybir.dt.from_np(_np.dtype(dtype))
        args.append(nc.dram_tensor(f"out_{i}_dram", shape, dt, kind="ExternalOutput").ap())
    conv_attention_moe_kernel(nc, *args)
    r = _run(nc, [arrays], core_ids=[0])
    got = tuple(r.results[0][f"out_{i}_dram"] for i in range(len(_OUTS)))
    return got[0]
```

```python
import concourse.bass as bass
from concourse import mybir
from contextlib import ExitStack


def conv_attention_moe_kernel(
    nc: bass.Bass,
    x: bass.AP,
    wf: bass.AP, bf: bass.AP, gf: bass.AP, betaf: bass.AP, mf: bass.AP, vf: bass.AP,
    wg: bass.AP, bg: bass.AP, gg: bass.AP, betag: bass.AP, mg: bass.AP, vg: bass.AP,
    wh: bass.AP, bh: bass.AP, wv: bass.AP, bv: bass.AP,
    Wk: bass.AP, bk: bass.AP, Wq: bass.AP, bq: bass.AP, Wv: bass.AP, bvalue: bass.AP,
    Wgate: bass.AP, W1: bass.AP, W2: bass.AP,
    out: bass.AP,
):
    fp32 = mybir.dt.float32
    fp16 = mybir.dt.float16
    bf16 = mybir.dt.bfloat16
    u32 = mybir.dt.uint32
    ALU = mybir.AluOpType
    ACT = mybir.ActivationFunctionType
    AX = mybir.AxisListType

    B, C, H, W = x.shape
    N = H * W
    P = 128
    A = N // P
    T = B * A
    MID = wf.shape[0]
    E, _, F = W1.shape
    FC = F // P
    NH = 2
    HBT = B // NH
    HT = T // NH
    HN = HT * P
    TOPS = 8
    BN_EPS = 1e-5
    LN_EPS = 1e-5
    NEG = -1e30
    XS = 16.0
    WS = 256.0

    x_v = x.rearrange("b c h w -> c b (h w)")
    out_v = out.rearrange("b c h w -> c b (h w)")
    gates_dram = nc.dram_tensor("gates_dram", [NH, E, HN], fp32).ap()

    def row(v, n=1):
        return v.rearrange("(a n) -> a n", a=n)

    def half(h):
        return slice(h * HBT, (h + 1) * HBT)

    SUMS = NH * E
    LAG = 3
    HB = 4
    POOL_WEIGHTS = 2
    POOL_LOW = ((0, 1, 2), (0, 2))

    TENSOR_ORDER = """
        tokens:0 convsT:0 bnT:0 convs:0 convs:1 convs:2 foldT:0 convs:3 scores:0 fold:0
        scores:1 tokens:1 probsT:0 branch:0 scores:2 probsT:1 scores:3 mix:0 mix:1 probsT:2
        branch:1 probsT:3 normT:0 mix:2 normT:1 mix:3 keys:0 values:0 keys:1 logits:0
        normT:2 values:1 logits:1 normT:3 keys:2 values:2 read:0 logits:2 keys:3 read:1
        values:3 logits:3 finalT:0 read:2 finalT:1 read:3 route:0 unit:0 unit:1 unit:2
        finalT:2 unit:3 gatesT:0 unit:4 unit:5 unit:6 unit:7 unit:8 finalT:3 unit:9 unit:10
        unit:11 route:1 unit:12 unit:13 unit:14 unit:15 unit:16 unit:17 unit:18 unit:19
        gatesT:1 unit:20 unit:21 unit:22 unit:23 unit:24 unit:25 unit:26 unit:27 unit:28
        unit:29 unit:30 unit:31"""
    SCALAR_ORDER = """
        tokens_high:0 tokens_high:1 relus:0 relus:1 relus:2 tokens_copy:0 relus:3 exp0:0
        tokens_copy:1 attention_high:0 exp0:1 probsT_copy:0 branch_copy:0 probsT_copy:1
        exp0:2 exp0:3 probsT_copy:2 branch_copy:1 value_bias_high:0 probsT_copy:3
        norm_high:0 weights:0 norm_high:1 keys_copy:0 keys_copy:1 norm_high:2 exp1:0
        norm_high:3 keys_copy:2 exp1:1 weights:1 keys_copy:3 exp1:2 weights:2 exp1:3
        final_copy:0 final_copy:1 unit:0 unit:1 tanh:0 unit:2 weights:3 final_copy:2 unit:3
        gatesT_copy:0 unit:4 unit:5 weights:4 unit:6 unit:7 weights:5 unit:8 final_copy:3
        weights:6 unit:9 unit:10 unit:11 unit:12 unit:13 unit:14 unit:15 unit:16 unit:17
        weights:7 tanh:1 unit:18 unit:19 gatesT_copy:1 unit:20 unit:21 unit:22 unit:23
        unit:24 unit:25 unit:26 unit:27 unit:28 unit:29 unit:30 unit:31"""
    VECTOR_ORDER = """
        convs_copy:0 tokens_split:0 bn_copy:0 bn_fold:0 tokens_split:1 branches_high:0
        branches_high:1 fold_prepare:0 branches_high:2 max0:0 fold_copy:0 max0:1
        branches_high:3 rec0:0 attention_low:0 max0:2 max0:3 rec0:1 add0:0 stats0:0 aggr0:0
        add0:1 stats0:1 rec0:2 aggr0:1 norm0:0 rec0:3 value_bias_low:0 norm0:1 normT_copy:0
        add0:2 stats0:2 normT_copy:1 aggr0:2 add0:3 stats0:3 aggr0:3 norm0:2 max1:0 norm0:3
        normT_copy:2 rec1:0 scale_values:0 max1:1 normT_copy:3 add1:0 rec1:1 scale_values:1
        stats1:0 max1:2 aggr1:0 add1:1 stats1:1 aggr1:1 rec1:2 norm1:0 max1:3 scale_values:2
        norm1:1 rec1:3 scale_values:3 add1:2 tokens_low:0 stats1:2 tokens_low:1 aggr1:2
        route_copy:0 add1:3 top_two:0 norm1:2 unit:0 unit:1 one_hots:0 gate_tokens:0 unit:2
        stats1:3 aggr1:3 weights_low:2 unit:3 norm1:3 unit:4 tokens_low:2 unit:5
        weights_low:3 unit:6 unit:7 unit:8 tokens_low:3 unit:9 unit:10 unit:11 route_copy:1
        unit:12 weights_low:4 top_two:1 unit:13 unit:14 unit:15 unit:16 one_hots:1
        weights_low:5 unit:17 gate_tokens:1 unit:18 unit:19 weights_low:6 unit:20 unit:21
        unit:22 weights_low:7 unit:23 unit:24 unit:25 unit:26 unit:27 unit:28 unit:29
        unit:30 unit:31"""
    GPSIMD_ORDER = """
        bn_pow:0 branches_low:0 branches_low:1 branches_low:2 branches_low:3 weights_scale:0
        rstd0:0 rstd0:1 residual:0 residual:1 rstd0:2 rstd0:3 weights_scale:1
        first_weights_low:0 rstd1:0 rstd1:1 residual:2 residual:3 first_weights_low:1
        rstd1:2 unit:0 unit:1 unit:2 rstd1:3 unit:3 unit:4 unit:5 unit:6 unit:7 unit:8
        unit:9 unit:10 unit:11 unit:12 unit:13 unit:14 unit:15 unit:16 unit:17 unit:18
        unit:19 unit:20 unit:21 unit:22 unit:23 unit:24 unit:25 unit:26 unit:27 unit:28
        unit:29 unit:30 unit:31"""
    WARM_UP = 4

    def in_order(order):
        for word in order.split():
            step, k = word.split(":")
            yield step, int(k)

    ctx = ExitStack()
    with ctx:
        def sb(name, shape, dt=fp32):
            return ctx.enter_context(nc.sbuf_tensor(name, shape, dt))

        def sem(name):
            return ctx.enter_context(nc.semaphore(name))

        xT = sb("xT", [P, B, N])
        bn_rows = sb("bn_rows", [10, MID])
        bn_cols = sb("bn_cols", [3 * MID, 10])
        bias_rows = sb("bias_rows", [2, P])
        bh_row = sb("bh_row", [1, MID])
        bias_cols = sb("bias_cols", [P, 3])
        wf_s = sb("wf_s", [MID, P])
        wg_s = sb("wg_s", [MID, P])
        wh_s = sb("wh_s", [MID, P])
        wv_s = sb("wv_s", [P, MID])
        MK = 3 * MID
        wfgT = sb("wfgT", [P, 2, 3, MID])
        wfgTh = sb("wfgTh", [P, 2, MK], fp16)
        wfgTl = sb("wfgTl", [P, 2, MK], fp16)
        xh = sb("xh", [P, B, N], fp16)
        xl = sb("xl", [P, B, N], fp16)
        wvT = sb("wvT", [MID, P])
        bv_row = sb("bv_row", [1, P])
        bvalue_row = sb("bvalue_row", [1, P])
        fold_bias = sb("fold_bias", [1, P])
        sixteen = sb("sixteen", [1, P], fp16)
        value_bias_h = sb("value_bias_h", [1, P], fp16)
        value_bias_l = sb("value_bias_l", [1, P], fp16)
        foldh = sb("foldh", [P, P], fp16)
        foldl = sb("foldl", [P, P], fp16)
        ident = sb("ident", [P, P])
        identb = sb("identb", [P, P], bf16)
        maskb = sb("maskb", [P, P], bf16)
        warm_b = sb("warm_b", [P, 512], bf16)
        ones = sb("ones", [1, P])
        iota_e = sb("iota_e", [P, E])
        power = sb("power", [P, 2])
        qscale = sb("qscale", [P, 2])
        bn_var = sb("bn_var", [MK, 2])
        bn_inv = sb("bn_inv", [MK, 2])
        bn_gain = sb("bn_gain", [MK, 2])
        bn_scale = sb("bn_scale", [MK, 2])
        bn_off = sb("bn_off", [MK, 2])
        bn_move = sb("bn_move", [MK, 2])
        bn_beta = sb("bn_beta", [MK, 2])
        bn_bias = sb("bn_bias", [MK, 2])
        bn_scale_w = sb("bn_scale_w", [MK, 2])
        fg = sb("fg", [MK, 2, 2, N])
        fg3 = sb("fg3", [MK, B, 2, N], fp16)
        hv = sb("hv", [P, T, P])
        xb = sb("xb", [P, T, P])
        nmax0 = sb("nmax0", [P, T])
        sum0 = sb("sum0", [P, T])
        rec0 = sb("rec0", [P, T])
        prob0 = sb("prob0", [P, T, N])
        prob0T = sb("prob0T", [P, T, N])
        t0 = xb
        st0 = sb("st0", [P, T, 6])
        mv0 = sb("mv0", [P, T, 2])
        ve0 = sb("ve0", [P, T])
        rstd0 = sb("rstd0", [P, T])
        y = sb("y", [P, T, P])
        ty = sb("ty", [P, T, P])
        yTh = sb("yTh", [P, B, N], fp16)
        yTl = sb("yTl", [P, B, N], fp16)
        aw = sb("aw", [P, 3 * P + E])
        awh = sb("awh", [P, 3 * P + E], fp16)
        awl = sb("awl", [P, 3 * P + E], fp16)
        kT = sb("kT", [P, B, N])
        qT = sb("qT", [P, B, N])
        vals = sb("vals", [P, T, P])
        LW = N + (A - 1) * P
        nmax1 = sb("nmax1", [P, T])
        sum1 = sb("sum1", [P, T])
        rec1 = sb("rec1", [P, T])
        prob1 = sb("prob1", [P, B, LW])
        t1 = sb("t1", [P, T, P])
        st1 = sb("st1", [P, T, 6])
        mv1 = sb("mv1", [P, T, 2])
        ve1 = sb("ve1", [P, T])
        rstd1 = sb("rstd1", [P, T])
        z = sb("z", [P, T, P])
        acc = sb("acc", [P, B, N])
        zh = sb("zh", [P, B, N], fp16)
        zl = sb("zl", [P, B, N], fp16)
        rl = sb("rl", [P, T, E])
        top = sb("top", [P, T, TOPS])
        topi = sb("topi", [P, T, TOPS], u32)
        topf = sb("topf", [P, T, 2])
        gap = sb("gap", [P, T, 1])
        tanh = sb("tanh", [P, T, 1])
        g1 = sb("g1", [P, T, 1])
        g2 = sb("g2", [P, T, 1])
        oh1 = sb("oh1", [P, T, E])
        oh2 = sb("oh2", [P, T, E])
        gw1 = sb("gw1", [P, T, E])
        gw2 = sb("gw2", [P, T, E])
        gate = sb("gate", [P, T, E])
        gateT = sb("gateT", [E, NH, HN])
        gates = sb("gates", [P, E, HN])
        W1f = sb("W1f", [P, E, F])
        W2f = sb("W2f", [P, E, F])
        W1h = sb("W1h", [P, E, F], fp16)
        W1l = sb("W1l", [P, E, F], fp16)
        W2h = sb("W2h", [P, E, F], fp16)
        W2l = sb("W2l", [P, E, F], fp16)
        hid = sb("hid", [P, HB, HN])
        hidh = sb("hidh", [P, HB, HN], fp16)
        hidl = sb("hidl", [P, HB, HN], fp16)
        gated = sb("gated", [P, 2, HN])
        gate_tiles = [gates, W1f]

        bank = [ctx.enter_context(nc.psum_tensor(f"bank{i}", [P, 512], fp32)) for i in range(8)]
        pS = pPT = pU = pYT = pKQ = pL = pR = pZ = bank[0:4]
        pV = [bank[4], bank[5], bank[4], bank[5]]
        pFG = bank[0:4]
        pX = [bank[5], bank[4]]
        pHV = [bank[6], bank[6]]
        pRT = [bank[6], bank[2]]
        pCT = [bank[7], bank[3]]
        pWF, pBN, pWV, pFOLD = bank[2], bank[3], bank[4], bank[6]
        pWARM = bank[7]
        pUP = [bank[0], bank[1]]
        pDN = [bank[6], bank[7]]

        x_in = [sem(f"x_in{h}") for h in range(NH)]
        wfg_in = sem("wfg_in")
        bn_in = sem("bn_in")
        bn_g_in = sem("bn_g_in")
        bias_in = sem("bias_in")
        wvh_in = sem("wvh_in")
        bias_row_in = sem("bias_row_in")
        attnw_in = sem("attnw_in")
        w_in = [sem(f"w_in{e}") for e in range(E)]
        zero_set = sem("zero_set")
        warm_set = sem("warm_set")
        ident_set = sem("ident_set")
        mask_set = sem("mask_set")
        ones_set = sem("ones_set")
        consts_set = sem("consts_set")
        iota_set = sem("iota_set")
        wfT_done = sem("wfT_done")
        wfT_ready = sem("wfT_ready")
        bnT_done = sem("bnT_done")
        bn_cols_ready = sem("bn_cols_ready")
        wvT_done = sem("wvT_done")
        wvT_ready = sem("wvT_ready")
        fold_done = sem("fold_done")
        bn_var_ready = sem("bn_var_ready")
        bn_inv_ready = sem("bn_inv_ready")
        bn_step = sem("bn_step")
        bn_ready = sem("bn_ready")
        xT_done = sem("xT_done")
        xb_ready = sem("xb_ready")
        fg_done = sem("fg_done")
        fg_ready = sem("fg_ready")
        fgh_ready = sem("fgh_ready")
        fg3_ready = sem("fg3_ready")
        xh_ready = sem("xh_ready")
        xl_ready = sem("xl_ready")
        foldh_ready = sem("foldh_ready")
        foldl_ready = sem("foldl_ready")
        fold_bias_ready = sem("fold_bias_ready")
        wfg_step = sem("wfg_step")
        awh_ready = sem("awh_ready")
        awl_ready = sem("awl_ready")
        hv_done = sem("hv_done")
        hv_ready = sem("hv_ready")
        s_done = sem("s_done")
        nmax0_ready = sem("nmax0_ready")
        prob0_ready = sem("prob0_ready")
        rec0_ready = sem("rec0_ready")
        pT_done = sem("pT_done")
        prob0T_ready = sem("prob0T_ready")
        u_done = sem("u_done")
        t0_ready = sem("t0_ready")
        st0_ready = sem("st0_ready")
        mv0_ready = sem("mv0_ready")
        ve0_ready = sem("ve0_ready")
        rstd0_ready = sem("rstd0_ready")
        y_ready = sem("y_ready")
        ty_ready = sem("ty_ready")
        yT_done = sem("yT_done")
        yTh_ready = sem("yTh_ready")
        yTl_ready = sem("yTl_ready")
        kq_done = sem("kq_done")
        kq_ready = sem("kq_ready")
        v_done = sem("v_done")
        value_bias_h_ready = sem("value_bias_h_ready")
        value_bias_l_ready = sem("value_bias_l_ready")
        sixteen_set = sem("sixteen_set")
        l_done = sem("l_done")
        nmax1_ready = sem("nmax1_ready")
        prob1_ready = sem("prob1_ready")
        rec1_ready = sem("rec1_ready")
        vals_ready = sem("vals_ready")
        r_done = sem("r_done")
        t1_ready = sem("t1_ready")
        st1_ready = sem("st1_ready")
        mv1_ready = sem("mv1_ready")
        ve1_ready = sem("ve1_ready")
        rstd1_ready = sem("rstd1_ready")
        z_ready = sem("z_ready")
        zT_done = sem("zT_done")
        acc_ready = sem("acc_ready")
        zh_ready = sem("zh_ready")
        zl_ready = sem("zl_ready")
        rt_done = sem("rt_done")
        rl_ready = sem("rl_ready")
        top_ready = sem("top_ready")
        topi_ready = sem("topi_ready")
        topf_ready = sem("topf_ready")
        gap_ready = sem("gap_ready")
        tanh_ready = sem("tanh_ready")
        g_ready = sem("g_ready")
        oh_ready = sem("oh_ready")
        gw_ready = sem("gw_ready")
        gate_ready = sem("gate_ready")
        gateT_done = sem("gateT_done")
        gateT_ready = sem("gateT_ready")
        gates_out = [sem(f"gates_out{h}") for h in range(NH)]
        gates_in = [sem(f"gates_in{d}") for d in range(SUMS)]
        wh_ready = sem("wh_ready")
        wl_ready = sem("wl_ready")
        ws_ready = sem("ws_ready")
        wl_pool = sem("wl_pool")
        up_done = sem("up_done")
        hid_ready = sem("hid_ready")
        high_ready = sem("high_ready")
        low_pool = sem("low_pool")
        low_dve = sem("low_dve")
        down_done = sem("down_done")
        gated_ready = sem("gated_ready")
        acc_added = sem("acc_added")
        out_stored = sem("out_stored")

        block = ctx.enter_context(nc.Block())

        def low_part(h, e, c):
            by_pool = c in POOL_LOW[h]
            per = [len(chunks) if by_pool else FC - len(chunks) for chunks in POOL_LOW]
            return (low_pool if by_pool else low_dve,
                    h * E * per[0] + e * per[h] + sum((q in POOL_LOW[h]) == by_pool for q in range(c + 1)))

        def unit_before(h, e, c, back):
            c -= back
            while c < 0:
                c += FC
                if isinstance(e, int) and e == 0:
                    if h == 0:
                        return None
                    h, e = h - 1, E - 1
                else:
                    e = e - 1
            return h, e, c

        def experts_of_second_half(eng, unit):
            for e in range(2):
                for c in range(FC):
                    unit(1, e, c, e)
            with eng.Fori(2, E - 1, 2) as e:
                for j in range(2):
                    for c in range(FC):
                        unit(1, e + j, c, j)

        BN_IN = 16 * 7
        BN_G_IN = 16 * 3
        BIAS_IN = 16 * 3
        ATTNW_IN = 16 * 4

        @block.sync
        def _(sync):
            sync.dma_start(xT[:, half(0), :], x_v[:, half(0), :]).then_inc(x_in[0], 16)
            sync.dma_start(wf_s[:, :], wf).then_inc(wfg_in, 16)
            for k, v in enumerate((bf, gf, betaf, mf, vf, bg, gg)):
                sync.dma_start(bn_rows[k:k + 1, :], row(v)).then_inc(bn_in, 16)
            sync.dma_start(xT[:, half(1), :], x_v[:, half(1), :]).then_inc(x_in[1], 16)
            sync.dma_start(wv_s[:, :], wv).then_inc(wvh_in, 16)
            sync.dma_start(wh_s[:, :], wh).then_inc(wvh_in, 16)
            sync.dma_start(bh_row[:, :], row(bh)).then_inc(bias_in, 16)
            sync.dma_start(bv_row[:, :], row(bv)).then_inc(bias_row_in, 16)
            sync.dma_start(bvalue_row[:, :], row(bvalue)).then_inc(bias_row_in, 16)
            sync.dma_start(bias_rows[0:1, :], row(bk)).then_inc(bias_in, 16)
            sync.dma_start(bias_rows[1:2, :], row(bq)).then_inc(bias_in, 16)
            for k, w in enumerate((Wk, Wq, Wv, Wgate)):
                sync.dma_start(aw[:, k * P:k * P + w.shape[1]], w).then_inc(attnw_in, 16)
            for e in range(E):
                sync.dma_start(W1f[:, e, :], W1[e, :, :]).then_inc(w_in[e], 16)
                sync.dma_start(W2f[:, e, :].rearrange("p (c d) -> p c d", c=FC),
                               W2[e, :, :].rearrange("(c p) d -> p c d", p=P)).then_inc(w_in[e], 16)
            for h in range(NH):
                sync.wait_ge(gateT_ready, h + 1)
                sync.dma_start(gates_dram[h, :, :], gateT[:, h, :]).then_inc(gates_out[h], 16)
                sync.wait_ge(gates_out[h], 16)
                if h == 1:
                    sync.wait_ge(wl_ready, 2 * (E - POOL_WEIGHTS))
                    sync.wait_ge(wl_pool, 2 * POOL_WEIGHTS)
                for e in range(E):
                    sync.dma_start(gate_tiles[h][:, e, :],
                                   gates_dram[h, e:e + 1, :].broadcast_to([P, HN])).then_inc(gates_in[h * E + e], 16)
            sync.wait_ge(acc_added, E)
            sync.dma_start(out_v[:, half(0), :], acc[:, half(0), :]).then_inc(out_stored, 16)
            for k in range(HBT):
                sync.wait_ge(acc_added, SUMS + k)
                sync.dma_start(out_v[:, HBT + k, :], acc[:, HBT + k, :]).then_inc(out_stored, 16)
            sync.wait_ge(out_stored, 16 * (1 + HBT))

        @block.gpsimd
        def _(pool):
            pool.memset(warm_b[:, :], 0.0).then_inc(warm_set, 1)
            pool.memset(ident[:, :], 0.0).then_inc(zero_set, 1)
            pool.wait_ge(zero_set, 1)
            pool.affine_select(out=ident[:, :], in_=ident[:, :], compare_op=ALU.not_equal, fill=1.0,
                               base=0, pattern=[[-1, P]], channel_multiplier=1).then_inc(ident_set, 1)
            for k, v in enumerate((betag, mg, vg)):
                pool.dma_start(bn_rows[7 + k:8 + k, :], row(v)).then_inc(bn_g_in, 16)
            pool.memset(power[:, :], -0.5).then_inc(consts_set, 1)
            pool.memset(qscale[:, 0:1], float(MID) ** -0.5).then_inc(consts_set, 1)
            pool.memset(qscale[:, 1:2], 1.0).then_inc(consts_set, 1)
            pool.memset(ones[:, :], 1.0).then_inc(ones_set, 1)
            pool.memset(sixteen[:, :], XS).then_inc(sixteen_set, 1)
            pool.memset(identb[:, :], 0.0).then_inc(zero_set, 1)
            pool.memset(maskb[:, :], 0.0).then_inc(zero_set, 1)
            pool.wait_ge(zero_set, 3)
            pool.affine_select(out=identb[:, :], in_=identb[:, :], compare_op=ALU.not_equal, fill=1.0,
                               base=0, pattern=[[-1, P]], channel_multiplier=1).then_inc(ident_set, 1)
            pool.affine_select(out=maskb[:, :], in_=maskb[:, :], compare_op=ALU.is_ge, fill=NEG,
                               base=0, pattern=[[1, P]], channel_multiplier=-1).then_inc(mask_set, 1)
            pool.iota(iota_e[:, :], pattern=[[1, E]], base=0, channel_multiplier=0,
                      allow_small_or_imprecise_dtypes=True).then_inc(iota_set, 1)

            def bn_pow(_):
                par = bn_cols[:, :].rearrange("p (w k) -> p w k", k=5)
                pool.wait_ge(bn_cols_ready, 1)
                pool.wait_ge(consts_set, 3)
                pool.tensor_scalar(bn_var[:, :], par[:, :, 4], BN_EPS, None, ALU.add).then_inc(bn_var_ready, 1)
                pool.wait_ge(bn_var_ready, 1)
                pool.tensor_tensor(bn_inv[:, :], bn_var[:, :], power[0:MK, :], ALU.pow).then_inc(bn_inv_ready, 1)

            def rstd(b, mv, ve, rs, mv_ready, ve_ready, rs_ready):
                r = slice(A * b, A * b + A)
                pool.wait_ge(mv_ready, b + 1)
                pool.tensor_scalar(ve[:, r], mv[:, r, 1], LN_EPS, None, ALU.add).then_inc(ve_ready, 1)
                pool.wait_ge(ve_ready, b + 1)
                pool.tensor_tensor(rs[:, r], ve[:, r], power[:, 0:A], ALU.pow).then_inc(rs_ready, 1)

            def rstd_0(b):
                rstd(b, mv0, ve0, rstd0, mv0_ready, ve0_ready, rstd0_ready)

            def residual(b):
                r = slice(A * b, A * b + A)
                pool.wait_ge(y_ready, b + 1)
                pool.tensor_tensor(ty[:, r, :], t0[:, r, :], y[:, r, :], ALU.add).then_inc(ty_ready, 1)

            def rstd_1(b):
                rstd(b, mv1, ve1, rstd1, mv1_ready, ve1_ready, rstd1_ready)

            def unit(h, e, c, parity):
                if c not in POOL_LOW[h]:
                    return
                n = (h * E + e) * FC + c
                pool.wait_ge(high_ready, n + 1)
                if unit_before(h, e, c, HB):
                    pool.wait_ge(down_done, n - HB + 1)
                pool.tensor_tensor(hidl[:, c, :], hid[:, c, :], hidh[:, c, :],
                                   ALU.subtract).then_inc(low_pool, 1)

            def branches_low(b):
                pool.wait_ge(fgh_ready, b + 1)
                for w, r in ((0, 2), (1, 1)):
                    q = slice(r * MID, (r + 1) * MID)
                    last = pool.tensor_tensor(fg3[q, b, w, :], fg[q, b % 2, w, :], fg3[q, b, w, :],
                                              ALU.subtract)
                last.then_inc(fg3_ready, 1)
                pool.wait_ge(fg3_ready, b + 1)

            def weights_scale(e):
                pool.wait_ge(w_in[e], 32)
                for w in (W1f, W2f):
                    pool.tensor_scalar(w[:, e, :], w[:, e, :], WS, None, ALU.mult).then_inc(ws_ready, 1)

            def first_weights_low(e):
                for k, (wl, w, whi) in enumerate(((W1l, W1f, W1h), (W2l, W2f, W2h))):
                    pool.wait_ge(wh_ready, 2 * e + k + 1)
                    pool.tensor_tensor(wl[:, e, :], w[:, e, :], whi[:, e, :],
                                       ALU.subtract).then_inc(wl_pool, 1)

            steps = {"weights_scale": weights_scale, "first_weights_low": first_weights_low,
                     "branches_low": branches_low, "bn_pow": bn_pow, "rstd0": rstd_0,
                     "residual": residual, "rstd1": rstd_1,
                     "unit": lambda n: unit(0, n // FC, n % FC, n // FC % 2)}
            for step, k in in_order(GPSIMD_ORDER):
                steps[step](k)
            experts_of_second_half(pool, unit)

        @block.scalar
        def _(act):
            act.dma_start(wg_s[:, :], wg).then_inc(wfg_in, 16)

            def tokens_high(h):
                act.wait_ge(x_in[h], 16)
                act.activation(xh[:, half(h), :], xT[:, half(h), :], ACT.Copy).then_inc(xh_ready, 1)

            def attention_high(_):
                act.wait_ge(attnw_in, ATTNW_IN)
                act.activation(awh[:, :], aw[:, :], ACT.Copy, scale=WS).then_inc(awh_ready, 1)

            def value_bias_high(_):
                act.wait_ge(bias_row_in, 32)
                act.activation(value_bias_h[:, :], bvalue_row[:, :], ACT.Copy,
                               scale=WS).then_inc(value_bias_h_ready, 1)

            def tokens_copy(h):
                r = slice(h * HT, (h + 1) * HT)
                act.wait_ge(xT_done, h + 1)
                act.activation(xb[:, r, :].rearrange("p t n -> p (t n)"), pX[h][:, :],
                               ACT.Copy).then_inc(xb_ready, 1)

            def branch_copy(h):
                r = slice(h * HT, (h + 1) * HT)
                act.wait_ge(hv_done, h + 1)
                act.activation(hv[:, r, :].rearrange("p t n -> p (t n)"), pHV[h][:, :], ACT.Copy,
                               scale=1.0 / WS).then_inc(hv_ready, 1)

            def relus(b):
                act.wait_ge(fg_done, b + 1)
                act.wait_ge(bn_ready, 1)
                if b >= 2:
                    act.wait_ge(fg3_ready, b - 1)
                for w in range(2):
                    last = act.activation(fg[:, b % 2, w, :], pFG[b][0:MK, w * N:(w + 1) * N], ACT.Relu,
                                          bias=bn_bias[0:MK, w:w + 1], scale=bn_scale_w[0:MK, w:w + 1])
                last.then_inc(fg_ready, 1)

            def exp_0(b):
                act.wait_ge(nmax0_ready, b + 1)
                for a in range(A):
                    i = A * b + a
                    act.activation(prob0[:, i, :], pS[b][:, a * N:(a + 1) * N], ACT.Exp,
                                   bias=nmax0[:, i:i + 1], accum_out=sum0[:, i:i + 1]).then_inc(prob0_ready, 1)

            def probsT_copy(b):
                act.wait_ge(pT_done, b + 1)
                act.activation(prob0T[:, A * b:A * b + A, :].rearrange("p a n -> p (a n)"),
                               pPT[b][:, :], ACT.Copy).then_inc(prob0T_ready, 1)

            def norm_high(b):
                act.wait_ge(yT_done, b + 1)
                act.activation(yTh[:, b, :], pYT[b][:, 0:N], ACT.Copy, scale=XS).then_inc(yTh_ready, 1)

            def keys_copy(b):
                act.wait_ge(kq_done, b + 1)
                act.activation(kT[:, b, :], pKQ[b][:, 0:N], ACT.Identity,
                               scale=1.0 / (XS * WS), bias=bias_cols[:, 0:1]).then_inc(kq_ready, 1)
                act.activation(qT[:, b, :], pKQ[b][:, N:2 * N], ACT.Identity,
                               scale=1.0 / (XS * WS), bias=bias_cols[:, 1:2]).then_inc(kq_ready, 1)

            def exp_1(b):
                act.wait_ge(nmax1_ready, A * (b + 1))
                for a in range(A):
                    i = A * b + a
                    lo, hi = (0, N) if a == 0 else (N, LW)
                    act.activation(prob1[:, b, lo:hi], pL[b][:, lo:hi], ACT.Exp,
                                   bias=nmax1[:, i:i + 1], accum_out=sum1[:, i:i + 1]).then_inc(prob1_ready, 1)

            def final_copy(b):
                act.wait_ge(zT_done, b + 1)
                act.activation(zh[:, b, :], pZ[b][:, 0:N], ACT.Copy, scale=XS).then_inc(zh_ready, 1)
                act.activation(acc[:, b, :], pZ[b][:, N:2 * N], ACT.Copy).then_inc(acc_ready, 1)

            def tanhs(h):
                act.wait_ge(gap_ready, h + 1)
                act.activation(tanh[:, h * HT:(h + 1) * HT, :], gap[:, h * HT:(h + 1) * HT, :],
                               ACT.Tanh, scale=0.5 / (XS * WS)).then_inc(tanh_ready, 1)

            def gatesT_copy(h):
                act.wait_ge(gateT_done, h + 1)
                act.activation(gateT[:, h, :], pCT[h][0:E, :], ACT.Copy).then_inc(gateT_ready, 1)

            def weights(e):
                for k, (whi, w) in enumerate(((W1h, W1f), (W2h, W2f))):
                    if e < POOL_WEIGHTS:
                        act.wait_ge(ws_ready, 2 * e + k + 1)
                    elif k == 0:
                        act.wait_ge(w_in[e], 32)
                    act.activation(whi[:, e, :], w[:, e, :], ACT.Copy,
                                   scale=1.0 if e < POOL_WEIGHTS else WS).then_inc(wh_ready, 1)

            def unit(h, e, c, parity):
                n = (h * E + e) * FC + c
                act.wait_ge(up_done, n + 1)
                if unit_before(h, e, c, HB):
                    act.wait_ge(*low_part(*unit_before(h, e, c, HB)))
                act.activation(hid[:, c, :], pUP[c % 2][:, :], ACT.Silu,
                               scale=1.0 / (XS * WS)).then_inc(hid_ready, 1)

            steps = {"tokens_high": tokens_high, "branch_copy": branch_copy, "tokens_copy": tokens_copy,
                     "attention_high": attention_high, "value_bias_high": value_bias_high, "norm_high": norm_high,
                     "relus": relus, "exp0": exp_0, "probsT_copy": probsT_copy, "keys_copy": keys_copy,
                     "exp1": exp_1, "final_copy": final_copy, "tanh": tanhs, "gatesT_copy": gatesT_copy,
                     "weights": weights,
                     "unit": lambda n: unit(0, n // FC, n % FC, n // FC % 2)}
            for step, k in in_order(SCALAR_ORDER):
                steps[step](k)
            experts_of_second_half(act, unit)

        @block.vector
        def _(dve):
            def convs_copy(_):
                dve.wait_ge(wfT_done, 1)
                src = pWF[:, 0:2 * MID].rearrange("p (w m) -> p w m", w=2)
                for r in range(3):
                    last = dve.tensor_scalar(wfgT[:, :, r, :], src, WS, None, ALU.mult)
                last.then_inc(wfg_step, 1)
                dve.wait_ge(wfg_step, 1)
                flat = wfgT[:, :, :, :].rearrange("p w r m -> p (w r m)")
                flath = wfgTh[:, :, :].rearrange("p w m -> p (w m)")
                flatl = wfgTl[:, :, :].rearrange("p w m -> p (w m)")
                dve.tensor_copy(flath, flat).then_inc(wfg_step, 1)
                dve.wait_ge(wfg_step, 2)
                dve.tensor_tensor(flatl, flat, flath, ALU.subtract).then_inc(wfT_ready, 1)

            def bn_copy(_):
                dve.wait_ge(bnT_done, 1)
                dve.tensor_copy(bn_cols[:, :], pBN[0:3 * MID, 0:10]).then_inc(bn_cols_ready, 1)
                dve.wait_ge(consts_set, 3)
                dve.wait_ge(bn_cols_ready, 1)
                par = bn_cols[:, :].rearrange("p (w k) -> p w k", k=5)
                dve.tensor_tensor(bn_gain[:, :], par[:, :, 1], qscale[0:MK, :], ALU.mult).then_inc(bn_step, 1)
                dve.tensor_tensor(bn_off[:, :], par[:, :, 0], par[:, :, 3], ALU.subtract).then_inc(bn_step, 1)
                dve.tensor_tensor(bn_beta[:, :], par[:, :, 2], qscale[0:MK, :], ALU.mult).then_inc(bn_step, 1)

            def bn_fold(_):
                dve.wait_ge(bn_inv_ready, 1)
                dve.wait_ge(bn_step, 3)
                dve.tensor_tensor(bn_scale[:, :], bn_inv[:, :], bn_gain[:, :], ALU.mult).then_inc(bn_step, 1)
                dve.wait_ge(bn_step, 4)
                dve.tensor_tensor(bn_move[:, :], bn_off[:, :], bn_scale[:, :], ALU.mult).then_inc(bn_step, 1)
                dve.wait_ge(bn_step, 5)
                dve.tensor_scalar(bn_scale_w[:, :], bn_scale[:, :], 1.0 / WS, None, ALU.mult).then_inc(bn_step, 1)
                dve.wait_ge(bn_step, 6)
                dve.tensor_tensor(bn_bias[:, :], bn_move[:, :], bn_beta[:, :], ALU.add).then_inc(bn_ready, 1)

            def tokens_split(h):
                dve.wait_ge(xh_ready, h + 1)
                dve.tensor_tensor(xl[:, half(h), :], xT[:, half(h), :], xh[:, half(h), :],
                                  ALU.subtract).then_inc(xl_ready, 1)

            def value_bias_low(_):
                dve.wait_ge(value_bias_h_ready, 1)
                dve.scalar_tensor_tensor(out=value_bias_l[:, :], in0=bvalue_row[:, :], scalar=WS,
                                         in1=value_bias_h[:, :], op0=ALU.mult,
                                         op1=ALU.subtract).then_inc(value_bias_l_ready, 1)

            def attention_low(_):
                dve.wait_ge(awh_ready, 1)
                dve.scalar_tensor_tensor(out=awl[:, :], in0=aw[:, :], scalar=WS, in1=awh[:, :],
                                         op0=ALU.mult, op1=ALU.subtract).then_inc(awl_ready, 1)

            def branches_high(b):
                dve.wait_ge(fg_ready, b + 1)
                dve.tensor_copy(fg3[:, b, :, :].rearrange("p w n -> p (w n)"),
                                fg[:, b % 2, :, :].rearrange("p w n -> p (w n)")).then_inc(fgh_ready, 1)

            def fold_prepare(_):
                dve.wait_ge(wvT_done, 1)
                dve.tensor_copy(bias_cols[:, 0:2], pWV[:, P:P + 2]).then_inc(wvT_ready, 1)
                dve.tensor_copy(bias_cols[0:MID, 2:3], pWV[0:MID, P + 2:P + 3]).then_inc(wvT_ready, 1)
                dve.tensor_copy(wvT[:, :], pWV[0:MID, 0:P]).then_inc(wvT_ready, 1)

            def fold_copy(_):
                dve.wait_ge(fold_done, 1)
                dve.tensor_scalar(foldh[:, :], pFOLD[:, 0:P], WS, None, ALU.mult).then_inc(foldh_ready, 1)
                dve.tensor_scalar(fold_bias[:, :], pFOLD[0:1, P:2 * P], WS, None, ALU.mult).then_inc(fold_bias_ready, 1)
                dve.wait_ge(foldh_ready, 1)
                dve.scalar_tensor_tensor(out=foldl[:, :], in0=pFOLD[:, 0:P], scalar=WS, in1=foldh[:, :],
                                         op0=ALU.mult, op1=ALU.subtract).then_inc(foldl_ready, 1)

            def max_0(b):
                dve.wait_ge(s_done, b + 1)
                dve.tensor_reduce(nmax0[:, A * b:A * b + A], pS[b][:, :].rearrange("p (a n) -> p a n", a=A),
                                  AX.X, ALU.max, negate=True).then_inc(nmax0_ready, 1)

            def stats(b, src, st, src_ready, count, st_ready):
                dve.wait_ge(src_ready, count)
                for i in range(A * b, A * b + A):
                    last = dve.bn_stats(st[:, i, :], src[:, i, :])
                last.then_inc(st_ready, 1)

            def aggregate(b, st, mv, st_ready, mv_ready):
                dve.wait_ge(st_ready, b + 1)
                for i in range(A * b, A * b + A):
                    last = dve.bn_aggr(mv[:, i, :], st[:, i, :])
                last.then_inc(mv_ready, 1)

            def normalize(b, src, mv, rs, dst, mv_ready, rs_ready, dst_ready):
                dve.wait_ge(mv_ready, b + 1)
                dve.wait_ge(rs_ready, b + 1)
                for i in range(A * b, A * b + A):
                    last = dve.tensor_scalar(dst[:, i, :], src[:, i, :], mv[:, i, 0:1], rs[:, i:i + 1],
                                             ALU.subtract, ALU.mult)
                last.then_inc(dst_ready, 1)

            def rec_0(b):
                dve.wait_ge(prob0_ready, A * (b + 1))
                dve.reciprocal(rec0[:, A * b:A * b + A], sum0[:, A * b:A * b + A]).then_inc(rec0_ready, 1)

            def add_0(b):
                dve.wait_ge(u_done, b + 1)
                dve.wait_ge(rec0_ready, b + 1)
                dve.wait_ge(xb_ready, b // HBT + 1)
                for a in range(A):
                    i = A * b + a
                    dve.scalar_tensor_tensor(out=t0[:, i, :], in0=pU[b][:, a * P:(a + 1) * P],
                                             scalar=rec0[:, i:i + 1], in1=xb[:, i, :],
                                             op0=ALU.mult, op1=ALU.add).then_inc(t0_ready, 1)

            def stats_0(b):
                stats(b, t0, st0, t0_ready, A * (b + 1), st0_ready)

            def aggr_0(b):
                aggregate(b, st0, mv0, st0_ready, mv0_ready)

            def norm_0(b):
                normalize(b, t0, mv0, rstd0, y, mv0_ready, rstd0_ready, y_ready)

            def normT_copy(b):
                dve.wait_ge(yTh_ready, b + 1)
                dve.scalar_tensor_tensor(out=yTl[:, b, :], in0=pYT[b][:, 0:N], scalar=XS, in1=yTh[:, b, :],
                                         op0=ALU.mult, op1=ALU.subtract).then_inc(yTl_ready, 1)

            def max_1(b):
                dve.wait_ge(l_done, b + 1)
                for a in range(A):
                    i = A * b + a
                    lo, hi = (0, N) if a == 0 else (N, LW)
                    dve.tensor_reduce(nmax1[:, i:i + 1], pL[b][:, lo:hi], AX.X, ALU.max,
                                      negate=True).then_inc(nmax1_ready, 1)

            def rec_1(b):
                dve.wait_ge(prob1_ready, A * (b + 1))
                dve.reciprocal(rec1[:, A * b:A * b + A], sum1[:, A * b:A * b + A]).then_inc(rec1_ready, 1)

            def scale_values(b):
                dve.wait_ge(rec1_ready, b + 1)
                dve.wait_ge(v_done, b + 1)
                for a in range(A):
                    i = A * b + a
                    last = dve.tensor_scalar(vals[:, i, :], pV[b][:, a * P:(a + 1) * P], rec1[:, i:i + 1],
                                             float(P) ** -0.5 / (XS * WS), ALU.mult, ALU.mult)
                last.then_inc(vals_ready, 1)

            def add_1(b):
                dve.wait_ge(r_done, b + 1)
                dve.wait_ge(ty_ready, b + 1)
                dve.tensor_tensor(t1[:, A * b:A * b + A, :].rearrange("p a n -> p (a n)"),
                                  pR[b][:, 0:A * P],
                                  ty[:, A * b:A * b + A, :].rearrange("p a n -> p (a n)"),
                                  ALU.add).then_inc(t1_ready, 1)

            def stats_1(b):
                stats(b, t1, st1, t1_ready, b + 1, st1_ready)

            def aggr_1(b):
                aggregate(b, st1, mv1, st1_ready, mv1_ready)

            def norm_1(b):
                normalize(b, t1, mv1, rstd1, z, mv1_ready, rstd1_ready, z_ready)

            def tokens_low(b):
                dve.wait_ge(zh_ready, b + 1)
                dve.wait_ge(acc_ready, b + 1)
                dve.scalar_tensor_tensor(out=zl[:, b, :], in0=pZ[b][:, 0:N], scalar=XS, in1=zh[:, b, :],
                                         op0=ALU.mult, op1=ALU.subtract).then_inc(zl_ready, 1)

            def route_copy(h):
                r = slice(h * HT, (h + 1) * HT)
                dve.wait_ge(rt_done, h + 1)
                dve.tensor_copy(rl[:, r, :].rearrange("p t e -> p (t e)"), pRT[h][:, 0:HT * E]).then_inc(rl_ready, 1)

            def top_two(h):
                r = slice(h * HT, (h + 1) * HT)
                dve.wait_ge(rl_ready, h + 1)
                for i in range(h * HT, (h + 1) * HT):
                    dve.max(top[:, i, :], rl[:, i, :]).then_inc(top_ready, 1)
                dve.wait_ge(top_ready, (h + 1) * HT)
                dve.tensor_tensor(gap[:, r, :], top[:, r, 1:2], top[:, r, 0:1], ALU.subtract).then_inc(gap_ready, 1)
                for i in range(h * HT, (h + 1) * HT):
                    dve.max_index(topi[:, i, :], top[:, i, :], rl[:, i, :]).then_inc(topi_ready, 1)

            def one_hots(h):
                r = slice(h * HT, (h + 1) * HT)
                dve.wait_ge(topi_ready, (h + 1) * HT)
                dve.tensor_copy(topf[:, r, :], topi[:, r, 0:2]).then_inc(topf_ready, 1)
                dve.wait_ge(topf_ready, h + 1)
                dve.wait_ge(iota_set, 1)
                lane = iota_e[:, :].unsqueeze(1).broadcast_to([P, HT, E])
                dve.tensor_tensor(oh1[:, r, :], topf[:, r, 0:1].broadcast_to([P, HT, E]), lane,
                                  ALU.is_equal).then_inc(oh_ready, 1)
                dve.tensor_tensor(oh2[:, r, :], topf[:, r, 1:2].broadcast_to([P, HT, E]), lane,
                                  ALU.is_equal).then_inc(oh_ready, 1)

            def gate_tokens(h):
                r = slice(h * HT, (h + 1) * HT)
                dve.wait_ge(tanh_ready, h + 1)
                dve.tensor_scalar(g1[:, r, :], tanh[:, r, :], -0.5 / WS, 0.5 / WS, ALU.mult, ALU.add).then_inc(g_ready, 1)
                dve.tensor_scalar(g2[:, r, :], tanh[:, r, :], 0.5 / WS, 0.5 / WS, ALU.mult, ALU.add).then_inc(g_ready, 1)
                dve.wait_ge(g_ready, 2 * (h + 1))
                dve.wait_ge(oh_ready, 2 * (h + 1))
                dve.tensor_tensor(gw1[:, r, :], oh1[:, r, :], g1[:, r, :].broadcast_to([P, HT, E]),
                                  ALU.mult).then_inc(gw_ready, 1)
                dve.tensor_tensor(gw2[:, r, :], oh2[:, r, :], g2[:, r, :].broadcast_to([P, HT, E]),
                                  ALU.mult).then_inc(gw_ready, 1)
                dve.wait_ge(gw_ready, 2 * (h + 1))
                dve.tensor_tensor(gate[:, r, :], gw1[:, r, :], gw2[:, r, :], ALU.add).then_inc(gate_ready, 1)

            def weights_low(e):
                for k, (wl, w, whi) in enumerate(((W1l, W1f, W1h), (W2l, W2f, W2h))):
                    dve.wait_ge(wh_ready, 2 * e + k + 1)
                    dve.scalar_tensor_tensor(out=wl[:, e, :], in0=w[:, e, :], scalar=WS, in1=whi[:, e, :],
                                             op0=ALU.mult, op1=ALU.subtract).then_inc(wl_ready, 1)

            def gate_output(h, e, parity):
                d = h * E + e
                dve.wait_ge(down_done, (d + 1) * FC)
                dve.tensor_tensor(gated[:, parity, :], pDN[parity][:, :], gate_tiles[h][:, e, :],
                                  ALU.mult).then_inc(gated_ready, 1)

            def add_gated(h, e, parity):
                a = acc[:, half(h), :].rearrange("p b n -> p (b n)")
                dve.wait_ge(gated_ready, h * E + e + 1)
                dve.tensor_tensor(a, a, gated[:, parity, :], ALU.add).then_inc(acc_added, 1)

            def last_sum(h, e, parity):
                d = h * E + e
                dve.wait_ge(down_done, (d + 1) * FC)
                for k in range(HBT):
                    t = slice(k * N, (k + 1) * N)
                    dve.tensor_tensor(gated[:, parity, t], pDN[parity][:, t], gate_tiles[h][:, e, t],
                                      ALU.mult).then_inc(gated_ready, 1)
                for k in range(HBT):
                    dve.wait_ge(gated_ready, d + 1 + k)
                    dve.tensor_tensor(acc[:, h * HBT + k, :], acc[:, h * HBT + k, :],
                                      gated[:, parity, k * N:(k + 1) * N], ALU.add).then_inc(acc_added, 1)

            def unit(h, e, c, parity):
                n = (h * E + e) * FC + c
                dve.wait_ge(hid_ready, n + 1)
                if unit_before(h, e, c, HB):
                    dve.wait_ge(down_done, n - HB + 1)
                dve.tensor_copy(hidh[:, c, :], hid[:, c, :]).then_inc(high_ready, 1)
                if c not in POOL_LOW[h]:
                    dve.wait_ge(high_ready, n + 1)
                    dve.tensor_tensor(hidl[:, c, :], hid[:, c, :], hidh[:, c, :],
                                      ALU.subtract).then_inc(low_dve, 1)
                done = unit_before(h, e, c, LAG)
                if done and done[2] == FC - 1:
                    if isinstance(done[1], int):
                        dve.wait_ge(gates_in[done[0] * E + done[1]], 16)
                        if done[1] == 0:
                            dve.wait_ge(acc_ready, HBT * (done[0] + 1))
                    gate_output(done[0], done[1], 1 - parity)
                done = unit_before(h, e, c, LAG + 1)
                if done and done[2] == FC - 1:
                    add_gated(done[0], done[1], 1 - parity)

            steps = {"tokens_split": tokens_split, "value_bias_low": value_bias_low,
                     "attention_low": attention_low, "branches_high": branches_high,
                     "convs_copy": convs_copy, "bn_copy": bn_copy, "bn_fold": bn_fold,
                     "fold_prepare": fold_prepare, "fold_copy": fold_copy,
                     "max0": max_0, "rec0": rec_0, "add0": add_0,
                     "stats0": stats_0, "aggr0": aggr_0, "norm0": norm_0, "normT_copy": normT_copy,
                     "max1": max_1, "rec1": rec_1,
                     "scale_values": scale_values, "add1": add_1, "stats1": stats_1, "aggr1": aggr_1,
                     "norm1": norm_1, "tokens_low": tokens_low, "route_copy": route_copy,
                     "top_two": top_two, "one_hots": one_hots, "gate_tokens": gate_tokens,
                     "weights_low": weights_low,
                     "unit": lambda n: unit(0, n // FC, n % FC, n // FC % 2)}
            for step, k in in_order(VECTOR_ORDER):
                steps[step](k)
            for e in range(1, E):
                dve.wait_ge(gates_in[E + e], 16)
            experts_of_second_half(dve, unit)
            last_sum(1, E - 1, 1)

        @block.tensor
        def _(pe):
            def warm_up(count):
                pe.wait_ge(warm_set, 1)
                for _ in range(count):
                    pe.matmul(pWARM[:, :], warm_b[:, 0:P], warm_b[:, :], start=True, stop=True)

            def convsT(_):
                pe.wait_ge(ident_set, 1)
                pe.wait_ge(wfg_in, 32)
                pe.transpose(pWF[:, 0:MID], wf_s[:, :], ident[0:MID, 0:MID])
                pe.transpose(pWF[:, MID:2 * MID], wg_s[:, :], ident[0:MID, 0:MID]).then_inc(wfT_done, 1)

            def split_product(o, ah, al, bh_, bl_, last=True):
                pe.matmul(o, ah, bh_, start=True, stop=False)
                pe.matmul(o, ah, bl_, start=False, stop=False)
                return pe.matmul(o, al, bh_, start=False, stop=last)

            def convs(b):
                pe.wait_ge(wfT_ready, 1)
                pe.wait_ge(bn_cols_ready, 1)
                pe.wait_ge(xl_ready, b // HBT + 1)
                pe.wait_ge(xh_ready, b // HBT + 1)
                for w in range(2):
                    last = split_product(pFG[b][0:MK, w * N:(w + 1) * N], wfgTh[:, w, :], wfgTl[:, w, :],
                                         xh[:, b, :], xl[:, b, :])
                last.then_inc(fg_done, 1)

            def bnT(_):
                pe.wait_ge(ident_set, 1)
                pe.wait_ge(bn_in, BN_IN)
                pe.wait_ge(bn_g_in, BN_G_IN)
                for r in range(3):
                    last = pe.matmul(pBN[r * MID:(r + 1) * MID, 0:10], bn_rows[:, :], ident[0:10, 0:10],
                                     start=True, stop=True)
                last.then_inc(bnT_done, 1)

            def foldT(_):
                pe.wait_ge(ident_set, 1)
                pe.wait_ge(wvh_in, 32)
                pe.wait_ge(bias_in, BIAS_IN)
                pe.transpose(pWV[:, P:P + 2], bias_rows[0:2, :], ident[0:2, 0:2])
                pe.transpose(pWV[0:MID, P + 2:P + 3], bh_row[:, :], ident[0:1, 0:1])
                pe.transpose(pWV[0:MID, 0:P], wv_s[:, :], ident[:, :]).then_inc(wvT_done, 1)

            def fold_convs(_):
                pe.wait_ge(wvT_ready, 3)
                pe.matmul(pFOLD[:, 0:P], wh_s[:, :], wvT[:, :], start=True, stop=True)
                pe.wait_ge(ones_set, 1)
                pe.wait_ge(bias_row_in, 32)
                pe.matmul(pFOLD[0:1, P:2 * P], bias_cols[0:MID, 2:3], wvT[:, :], start=True, stop=False)
                pe.matmul(pFOLD[0:1, P:2 * P], ones[0:1, 0:1], bv_row[:, :], start=False,
                          stop=True).then_inc(fold_done, 1)

            def tokens(h):
                pe.wait_ge(ident_set, 1)
                pe.wait_ge(x_in[h], 16)
                if h == 1:
                    pe.wait_ge(wvT_ready, 3)
                for i in range(HT):
                    b, a = h * HBT + i // A, i % A
                    last = pe.transpose(pX[h][:, i * P:(i + 1) * P], xT[:, b, a * P:(a + 1) * P], ident[:, :])
                last.then_inc(xT_done, 1)

            def branch(h):
                if h == 1:
                    pe.wait_ge(hv_ready, 1)
                pe.wait_ge(foldl_ready, 1)
                pe.wait_ge(fold_bias_ready, 1)
                pe.wait_ge(xl_ready, h + 1)
                for i in range(HT):
                    b, t = h * HBT + i // A, slice(i % A * P, (i % A + 1) * P)
                    o = pHV[h][:, i * P:(i + 1) * P]
                    split_product(o, xh[:, b, t], xl[:, b, t], foldh[:, :], foldl[:, :], last=False)
                    last = pe.matmul(o, ones[0:1, :], fold_bias[:, :], start=False, stop=True)
                last.then_inc(hv_done, 1)

            def scores(b):
                pe.wait_ge(fg3_ready, b + 1)
                for a in range(A):
                    last = pe.matmul(pS[b][:, a * N:(a + 1) * N], fg3[:, b, 0, a * P:(a + 1) * P],
                                     fg3[:, b, 1, :], start=True, stop=True)
                last.then_inc(s_done, 1)

            def probsT(b):
                pe.wait_ge(prob0_ready, A * (b + 1))
                for j in range(A):
                    for a in range(A):
                        col = j * N + a * P
                        last = pe.transpose(pPT[b][:, col:col + P],
                                            prob0[:, A * b + a, j * P:(j + 1) * P], ident[:, :])
                last.then_inc(pT_done, 1)

            def mix(b):
                pe.wait_ge(prob0T_ready, b + 1)
                pe.wait_ge(hv_ready, b // HBT + 1)
                for a in range(A):
                    for j in range(A):
                        last = pe.matmul(pU[b][:, a * P:(a + 1) * P],
                                         prob0T[:, A * b + j, a * P:(a + 1) * P], hv[:, A * b + j, :],
                                         start=(j == 0), stop=(j == A - 1))
                last.then_inc(u_done, 1)

            def normT(b):
                pe.wait_ge(y_ready, b + 1)
                for a in range(A):
                    last = pe.transpose(pYT[b][:, a * P:(a + 1) * P], y[:, A * b + a, :], ident[:, :])
                last.then_inc(yT_done, 1)

            def keys(b):
                pe.wait_ge(awl_ready, 1)
                pe.wait_ge(yTl_ready, b + 1)
                split_product(pKQ[b][:, 0:N], awh[:, 0:P], awl[:, 0:P], yTh[:, b, :], yTl[:, b, :])
                split_product(pKQ[b][:, N:2 * N], awh[:, P:2 * P], awl[:, P:2 * P],
                              yTh[:, b, :], yTl[:, b, :]).then_inc(kq_done, 1)

            def values(b):
                pe.wait_ge(*((vals_ready, b - 1) if b >= 2 else (xb_ready, 2 - b)))
                pe.wait_ge(value_bias_l_ready, 1)
                pe.wait_ge(sixteen_set, 1)
                for a in range(A):
                    t = slice(a * P, (a + 1) * P)
                    split_product(pV[b][:, t], yTh[:, b, t], yTl[:, b, t],
                                  awh[:, 2 * P:3 * P], awl[:, 2 * P:3 * P], last=False)
                    pe.matmul(pV[b][:, t], sixteen[:, :], value_bias_h[:, :], start=False, stop=False)
                    last = pe.matmul(pV[b][:, t], sixteen[:, :], value_bias_l[:, :], start=False, stop=True)
                last.then_inc(v_done, 1)

            def logits(b):
                pe.wait_ge(mask_set, 1)
                pe.wait_ge(ident_set, 2)
                pe.wait_ge(kq_ready, 2 * (b + 1))
                for a in range(A):
                    lo, hi = (0, N) if a == 0 else (N, LW)
                    pe.matmul(pL[b][:, lo:hi], kT[:, b, a * P:(a + 1) * P], qT[:, b, a * P:N],
                              start=True, stop=False)
                    last = pe.matmul(pL[b][:, lo:lo + P], identb[:, :], maskb[:, :],
                                     start=False, stop=True)
                last.then_inc(l_done, 1)

            def read(b):
                pe.wait_ge(prob1_ready, A * (b + 1))
                pe.wait_ge(vals_ready, b + 1)
                pe.matmul(pR[b][:, 0:P], prob1[:, b, 0:P], vals[:, A * b, :], start=True, stop=True)
                pe.matmul(pR[b][:, P:2 * P], prob1[:, b, P:N], vals[:, A * b, :], start=True, stop=False)
                pe.matmul(pR[b][:, P:2 * P], prob1[:, b, N:LW], vals[:, A * b + 1, :], start=False,
                          stop=True).then_inc(r_done, 1)

            def finalT(b):
                pe.wait_ge(z_ready, b + 1)
                for a in range(A):
                    i = A * b + a
                    pe.transpose(pZ[b][:, a * P:(a + 1) * P], z[:, i, :], ident[:, :])
                    last = pe.transpose(pZ[b][:, N + a * P:N + (a + 1) * P], t1[:, i, :], ident[:, :])
                last.then_inc(zT_done, 1)

            def route(h):
                pe.wait_ge(*((hv_ready, NH) if h == 0 else (zl_ready, B)))
                for i in range(HT):
                    b, a = h * HBT + i // A, i % A
                    pe.wait_ge(zl_ready, b + 1)
                    t = slice(a * P, (a + 1) * P)
                    last = split_product(pRT[h][:, i * E:(i + 1) * E], zh[:, b, t], zl[:, b, t],
                                         awh[:, 3 * P:3 * P + E], awl[:, 3 * P:3 * P + E])
                last.then_inc(rt_done, 1)

            def gatesT(h):
                pe.wait_ge(gate_ready, h + 1)
                for i in range(HT):
                    last = pe.transpose(pCT[h][0:E, i * P:(i + 1) * P], gate[:, h * HT + i, :], ident[:, :])
                last.then_inc(gateT_done, 1)

            def down(h, e, c, parity):
                if c == 0:
                    if isinstance(e, int) and h == 0 and e < 2:
                        pe.wait_ge(*((rl_ready, 1) if e == 0 else (gateT_ready, 1)))
                    else:
                        pe.wait_ge(gated_ready, h * E + e - 1)
                ch = slice(c * P, (c + 1) * P)
                o = pDN[parity][:, :]
                pe.wait_ge(high_ready, (h * E + e) * FC + c + 1)
                pe.matmul(o, W2h[:, e, ch], hidh[:, c, :], start=(c == 0), stop=False)
                pe.matmul(o, W2l[:, e, ch], hidh[:, c, :], start=False, stop=False)
                pe.wait_ge(*low_part(h, e, c))
                pe.matmul(o, W2h[:, e, ch], hidl[:, c, :], start=False,
                          stop=(c == FC - 1)).then_inc(down_done, 1)

            def unit(h, e, c, parity):
                if h == 0 and c == 0:
                    pe.wait_ge(*((wl_pool, 2 * e + 2) if e < POOL_WEIGHTS
                                 else (wl_ready, 2 * (e - POOL_WEIGHTS) + 2)))
                if isinstance(e, int) and e == 0 and c == 0:
                    pe.wait_ge(zl_ready, HBT * (h + 1))
                n = (h * E + e) * FC + c
                if unit_before(h, e, c, 2):
                    pe.wait_ge(hid_ready, n - 1)
                ch = slice(c * P, (c + 1) * P)
                th = zh[:, half(h), :].rearrange("p b n -> p (b n)")
                tl = zl[:, half(h), :].rearrange("p b n -> p (b n)")
                o = pUP[c % 2][:, :]
                pe.matmul(o, W1h[:, e, ch], th, start=True, stop=False)
                pe.matmul(o, W1h[:, e, ch], tl, start=False, stop=False)
                pe.matmul(o, W1l[:, e, ch], th, start=False, stop=True).then_inc(up_done, 1)
                m = unit_before(h, e, c, LAG)
                if m:
                    down(*m, parity if m[2] <= c else 1 - parity)

            steps = {"convsT": convsT, "convs": convs, "bnT": bnT, "foldT": foldT, "fold": fold_convs,
                     "tokens": tokens, "branch": branch, "scores": scores, "probsT": probsT, "mix": mix,
                     "normT": normT, "keys": keys, "values": values, "logits": logits,
                     "read": read, "finalT": finalT, "route": route, "gatesT": gatesT,
                     "unit": lambda n: unit(0, n // FC, n % FC, n // FC % 2)}
            warm_up(WARM_UP)
            for step, k in in_order(TENSOR_ORDER):
                steps[step](k)
            experts_of_second_half(pe, unit)
            for c in range(FC - LAG, FC):
                down(1, E - 1, c, (E - 1) % 2)


_INS = ['x', 'L0_conv_wf', 'L0_conv_bf', 'L0_conv_gf', 'L0_conv_betaf', 'L0_conv_mf', 'L0_conv_vf',
        'L0_conv_wg', 'L0_conv_bg', 'L0_conv_gg', 'L0_conv_betag', 'L0_conv_mg', 'L0_conv_vg',
        'L0_conv_wh', 'L0_conv_bh', 'L0_conv_wv', 'L0_conv_bv',
        'L1_attn_Wk', 'L1_attn_bk', 'L1_attn_Wq', 'L1_attn_bq', 'L1_attn_Wv', 'L1_attn_bv',
        'L1_ffn_Wg', 'L1_ffn_W1', 'L1_ffn_W2']
_OUTS = [((4, 128, 16, 16), 'float32')]


def kernel(**inputs):
    import numpy as _np
    import concourse.bacc as _bacc
    from concourse import mybir as _mybir
    from concourse.bass_utils import run_bass_kernel_spmd as _run

    nc = _bacc.Bacc("TRN2", target_bir_lowering=False, num_devices=1)
    arrays, args = {}, []
    for name in _INS:
        a = _np.ascontiguousarray(inputs[name])
        arrays[f"in_{name}_dram"] = a
        args.append(nc.dram_tensor(f"in_{name}_dram", a.shape, _mybir.dt.from_np(a.dtype), kind="ExternalInput").ap())
    for i, (shape, dtype) in enumerate(_OUTS):
        dt = _mybir.dt.from_np(_np.dtype(dtype))
        args.append(nc.dram_tensor(f"out_{i}_dram", shape, dt, kind="ExternalOutput").ap())
    conv_attention_moe_kernel(nc, *args)
    r = _run(nc, [arrays], core_ids=[0])
    got = tuple(r.results[0][f"out_{i}_dram"] for i in range(len(_OUTS)))
    return got[0]
```
